# Optimizing a Trainium2 kernel written in Bass

```python
import numpy as np
import jax
import jax.numpy as jnp

def _softmax(x, axis=-1):
    return jax.nn.softmax(x, axis=axis)

def _gelu(x):
    return jax.nn.gelu(x, approximate=True)

def _silu(x):
    return jax.nn.silu(x)

def _sigmoid(x):
    return jax.nn.sigmoid(x)

def _layernorm(x, axis=-1, eps=1e-05):
    m = jnp.mean(x, axis=axis, keepdims=True)
    v = jnp.var(x, axis=axis, keepdims=True)
    return (x - m) / jnp.sqrt(v + eps)

def _scatter_add(tgt, idx, src, axis=0):
    return tgt.at[idx].add(src)

def _segment_sum(src, seg, n):
    return jax.ops.segment_sum(src, seg, n)
kernel_name = 'mk_lm_tower_d1_tok_ids4096_r4_4f096e'

def setup_inputs(seed: int=0):
    np.random.seed(seed)
    _w = jnp.asarray

    def _rec_inputs():
        import jax
        import jax.numpy as jnp
        _rk = jax.random.key(seed)
        x = jax.random.randint(jax.random.fold_in(_rk, 1), (8, 512), 0, 12564, jnp.int32)
        return x
    x = _rec_inputs()

    def _L0_tok_setup():
        import jax, jax.numpy as jnp
        import numpy as np
        C, V, R, D = (8, 50257, 32, 1024)
        B, S = (4, 1024)
        key = jax.random.key(seed)
        k1, k2, k3, k4 = jax.random.split(key, 4)
        x = jax.random.randint(k1, (B, S), 0, V)
        probs = jax.random.uniform(k2, (C,), dtype=jnp.float32)
        E_in = jax.random.normal(k3, (C, V, R), dtype=jnp.float32) / np.float32(np.sqrt(R))
        W_out = jax.random.normal(k4, (C, D, R), dtype=jnp.float32) * np.float32(1.0 / np.sqrt(R))
        return {'x': x, 'probs': probs, 'E_in': E_in, 'W_out': W_out}
    _L0_tok_all = _L0_tok_setup()
    _L0_tok_in = {k: v for k, v in _L0_tok_all.items() if k in ('probs', 'E_in', 'W_out')}
    del _L0_tok_all

    def _L0_attn_setup():
        import jax, jax.numpy as jnp
        import numpy as np
        from jax import lax
        H = 1024
        DIN = 2048
        N = 16
        K = 4
        R = 64
        B_SZ = 2
        L = 512
        EPS = 1e-06

        def rmsnorm(x, w):
            return x * lax.rsqrt(jnp.mean(x * x, axis=-1, keepdims=True) + EPS) * w

        def _selective_scan(x, dt, A, Bm, Cm):
            xT = jnp.transpose(x, (2, 0, 1))
            dtT = jnp.transpose(dt, (2, 0, 1))
            BT = jnp.transpose(Bm, (2, 0, 1))
            CT = jnp.transpose(Cm, (2, 0, 1))

            def step(h, inp):
                x_t, dt_t, B_t, C_t = inp
                dA = jnp.exp(dt_t[..., None] * A)
                dBx = dt_t[..., None] * B_t[:, None, :] * x_t[..., None]
                h = dA * h + dBx
                y = jnp.einsum('bdn,bn->bd', h, C_t)
                return (h, y)
            h0 = jnp.zeros((x.shape[0], x.shape[1], A.shape[1]), dtype=x.dtype)
            _, ys = lax.scan(step, h0, (xT, dtT, BT, CT))
            return jnp.transpose(ys, (1, 2, 0))
        key = jax.random.key(seed)
        ks = jax.random.split(key, 8)
        hidden_states = jax.random.normal(ks[0], (B_SZ, L, H), dtype=jnp.float32)
        s = 0.02
        in_proj_w = jax.random.normal(ks[1], (H, 2 * DIN), dtype=jnp.float32) * s
        conv_w = jax.random.normal(ks[2], (DIN, K), dtype=jnp.float32) * 0.2
        conv_b = jax.random.normal(ks[3], (DIN,), dtype=jnp.float32) * 0.02
        x_proj_w = jax.random.normal(ks[4], (R + 2 * N, DIN), dtype=jnp.float32) * s
        dt_proj_w = jax.random.normal(ks[5], (DIN, R), dtype=jnp.float32) * s
        dt_bias = jax.random.normal(ks[6], (DIN,), dtype=jnp.float32) * 0.5 - 4.0
        A_log = jnp.log(jnp.broadcast_to(jnp.arange(1, N + 1, dtype=jnp.float32)[None, :], (DIN, N)))
        D_param = jnp.ones((DIN,), dtype=jnp.float32)
        out_proj_w = jax.random.normal(ks[7], (H, DIN), dtype=jnp.float32) * s
        dt_ln_w = jnp.ones((R,), dtype=jnp.float32)
        B_ln_w = jnp.ones((N,), dtype=jnp.float32)
        C_ln_w = jnp.ones((N,), dtype=jnp.float32)
        return dict(hidden_states=hidden_states, in_proj_w=in_proj_w, conv_w=conv_w, conv_b=conv_b, x_proj_w=x_proj_w, dt_proj_w=dt_proj_w, dt_bias=dt_bias, A_log=A_log, D_param=D_param, out_proj_w=out_proj_w, dt_ln_w=dt_ln_w, B_ln_w=B_ln_w, C_ln_w=C_ln_w)
    _L0_attn_all = _L0_attn_setup()
    _L0_attn_in = {k: v for k, v in _L0_attn_all.items() if k in ('in_proj_w', 'conv_w', 'conv_b', 'x_proj_w', 'dt_proj_w', 'dt_bias', 'A_log', 'D_param', 'out_proj_w', 'dt_ln_w', 'B_ln_w', 'C_ln_w')}
    del _L0_attn_all

    def _L0_ffn_setup():
        import jax, jax.numpy as jnp
        import numpy as np
        RANKS = (8, 16, 32, 64)
        TOPK = 1
        SCALING = 1.0 / 4
        key = jax.random.key(seed)
        ks = jax.random.split(key, 7)
        D_IN, D_OUT, MAX_R, N_RANKS = (1024, 1024, 64, len(RANKS))
        B_, S_ = (4, 512)
        return {'hidden_states': jax.random.normal(ks[0], (B_, S_, D_IN), jnp.float32), 'W': jax.random.normal(ks[1], (D_OUT, D_IN), jnp.float32) * 0.02, 'b': jax.random.normal(ks[2], (D_OUT,), jnp.float32) * 0.02, 'A': jax.random.normal(ks[3], (MAX_R, D_IN), jnp.float32) * 0.02, 'B': jnp.zeros((D_OUT, MAX_R), jnp.float32) + jax.random.normal(ks[4], (D_OUT, MAX_R), jnp.float32) * 0.02, 'gate_w': jax.random.normal(ks[5], (N_RANKS, D_IN), jnp.float32) * 0.02, 'gate_b': jax.random.normal(ks[6], (N_RANKS,), jnp.float32) * 0.02}
    _L0_ffn_all = _L0_ffn_setup()
    _L0_ffn_in = {k: v for k, v in _L0_ffn_all.items() if k in ('W', 'b', 'A', 'B', 'gate_w', 'gate_b')}
    del _L0_ffn_all
    return {'x': x, 'L0_tok_probs': _L0_tok_in['probs'], 'L0_tok_E_in': _L0_tok_in['E_in'], 'L0_tok_W_out': _L0_tok_in['W_out'], 'L0_attn_in_proj_w': _L0_attn_in['in_proj_w'], 'L0_attn_conv_w': _L0_attn_in['conv_w'], 'L0_attn_conv_b': _L0_attn_in['conv_b'], 'L0_attn_x_proj_w': _L0_attn_in['x_proj_w'], 'L0_attn_dt_proj_w': _L0_attn_in['dt_proj_w'], 'L0_attn_dt_bias': _L0_attn_in['dt_bias'], 'L0_attn_A_log': _L0_attn_in['A_log'], 'L0_attn_D_param': _L0_attn_in['D_param'], 'L0_attn_out_proj_w': _L0_attn_in['out_proj_w'], 'L0_attn_dt_ln_w': _L0_attn_in['dt_ln_w'], 'L0_attn_B_ln_w': _L0_attn_in['B_ln_w'], 'L0_attn_C_ln_w': _L0_attn_in['C_ln_w'], 'L0_ffn_W': _L0_ffn_in['W'], 'L0_ffn_b': _L0_ffn_in['b'], 'L0_ffn_A': _L0_ffn_in['A'], 'L0_ffn_B': _L0_ffn_in['B'], 'L0_ffn_gate_w': _L0_ffn_in['gate_w'], 'L0_ffn_gate_b': _L0_ffn_in['gate_b']}

def reference(x, L0_tok_probs, L0_tok_E_in, L0_tok_W_out, L0_attn_in_proj_w, L0_attn_conv_w, L0_attn_conv_b, L0_attn_x_proj_w, L0_attn_dt_proj_w, L0_attn_dt_bias, L0_attn_A_log, L0_attn_D_param, L0_attn_out_proj_w, L0_attn_dt_ln_w, L0_attn_B_ln_w, L0_attn_C_ln_w, L0_ffn_W, L0_ffn_b, L0_ffn_A, L0_ffn_B, L0_ffn_gate_w, L0_ffn_gate_b):
    import jax
    import jax.numpy as jnp

    def _L0_tok_ref(x, probs, E_in, W_out):
        import jax, jax.numpy as jnp
        import numpy as np
        C, V, R, D = (8, 50257, 32, 1024)
        B, S = (4, 1024)
        low = jnp.take(E_in, x, axis=1)
        return jnp.einsum('c,cbsr,cdr->bsd', probs, low, W_out)

    def _L0_attn_ref(hidden_states, in_proj_w, conv_w, conv_b, x_proj_w, dt_proj_w, dt_bias, A_log, D_param, out_proj_w, dt_ln_w, B_ln_w, C_ln_w):
        import jax, jax.numpy as jnp
        import numpy as np
        from jax import lax
        H = 1024
        DIN = 2048
        N = 16
        K = 4
        R = 64
        B_SZ = 2
        L = 512
        EPS = 1e-06

        def rmsnorm(x, w):
            return x * lax.rsqrt(jnp.mean(x * x, axis=-1, keepdims=True) + EPS) * w

        def _selective_scan(x, dt, A, Bm, Cm):
            xT = jnp.transpose(x, (2, 0, 1))
            dtT = jnp.transpose(dt, (2, 0, 1))
            BT = jnp.transpose(Bm, (2, 0, 1))
            CT = jnp.transpose(Cm, (2, 0, 1))

            def step(h, inp):
                x_t, dt_t, B_t, C_t = inp
                dA = jnp.exp(dt_t[..., None] * A)
                dBx = dt_t[..., None] * B_t[:, None, :] * x_t[..., None]
                h = dA * h + dBx
                y = jnp.einsum('bdn,bn->bd', h, C_t)
                return (h, y)
            h0 = jnp.zeros((x.shape[0], x.shape[1], A.shape[1]), dtype=x.dtype)
            _, ys = lax.scan(step, h0, (xT, dtT, BT, CT))
            return jnp.transpose(ys, (1, 2, 0))
        proj = hidden_states @ in_proj_w
        x, z = jnp.split(proj, 2, axis=-1)
        x = jnp.transpose(x, (0, 2, 1))
        z = jnp.transpose(z, (0, 2, 1))
        Lq = x.shape[-1]
        xp = jnp.pad(x, ((0, 0), (0, 0), (K - 1, 0)))
        xc = conv_b[None, :, None]
        for k in range(K):
            xc = xc + conv_w[None, :, k:k + 1] * xp[:, :, k:k + Lq]
        xc = jax.nn.silu(xc)
        ssm_p = jnp.einsum('bdl,ed->ble', xc, x_proj_w)
        dt_r = rmsnorm(ssm_p[..., :R], dt_ln_w)
        Bm = rmsnorm(ssm_p[..., R:R + N], B_ln_w)
        Cm = rmsnorm(ssm_p[..., R + N:], C_ln_w)
        dt = jnp.einsum('blr,dr->bdl', dt_r, dt_proj_w)
        dt = jax.nn.softplus(dt + dt_bias[None, :, None])
        A = -jnp.exp(A_log)
        Bm = jnp.transpose(Bm, (0, 2, 1))
        Cm = jnp.transpose(Cm, (0, 2, 1))
        ys = _selective_scan(xc, dt, A, Bm, Cm)
        y = (ys + D_param[None, :, None] * xc) * jax.nn.silu(z)
        return jnp.einsum('bdl,hd->blh', y, out_proj_w)

    def _L0_ffn_ref(hidden_states, W, b, A, B, gate_w, gate_b):
        import jax, jax.numpy as jnp
        import numpy as np
        RANKS = (8, 16, 32, 64)
        TOPK = 1
        SCALING = 1.0 / 4
        bsz, seq, d_in = hidden_states.shape
        out = jnp.einsum('bsd,od->bso', hidden_states, W) + b
        x = hidden_states.reshape(-1, d_in)
        scores = x @ gate_w.T + gate_b
        probs = jax.nn.softmax(scores, axis=-1)
        routing_weights, selected = jax.lax.top_k(probs, TOPK)
        routing_weights = routing_weights / jnp.sum(routing_weights, axis=-1, keepdims=True)
        lora_outputs = jnp.stack([x @ A[:r, :].T @ B[:, :r].T for r in RANKS], axis=1)
        sel = jnp.take_along_axis(lora_outputs, selected[:, :, None], axis=1)
        final = jnp.sum(sel * routing_weights[:, :, None], axis=1)
        return out + final.reshape(bsz, seq, -1)
    h = _L0_tok_ref(x, L0_tok_probs, L0_tok_E_in, L0_tok_W_out)
    h = h + _L0_attn_ref(_layernorm(h, axis=-1), L0_attn_in_proj_w, L0_attn_conv_w, L0_attn_conv_b, L0_attn_x_proj_w, L0_attn_dt_proj_w, L0_attn_dt_bias, L0_attn_A_log, L0_attn_D_param, L0_attn_out_proj_w, L0_attn_dt_ln_w, L0_attn_B_ln_w, L0_attn_C_ln_w)
    h = h + _L0_ffn_ref(_layernorm(h, axis=-1), L0_ffn_W, L0_ffn_b, L0_ffn_A, L0_ffn_B, L0_ffn_gate_w, L0_ffn_gate_b)
    return h

_drawn_inputs = setup_inputs


def setup_inputs(seed=0):
    import zlib

    import numpy as np

    out = dict(_drawn_inputs(seed))
    spreads = {'L0_attn_D_param': (1.0, 0.2),
     'L0_attn_dt_ln_w': (1.0, 0.6),
     'L0_attn_B_ln_w': (1.0, 0.2),
     'L0_attn_C_ln_w': (1.0, 0.6)}
    factors = {'L0_attn_dt_proj_w': 3.948, 'L0_ffn_gate_b': 4.22}
    for name, (base, spread) in spreads.items():
        noise = np.random.default_rng([zlib.crc32(name.encode()), seed]).standard_normal(out[name].shape)
        drawn = base * np.exp(spread * noise) if base else spread * noise
        out[name] = jnp.asarray(drawn.astype(out[name].dtype))
    for name, factor in factors.items():
        out[name] = (out[name] * factor).astype(out[name].dtype)
    return out
```

```python
from contextlib import ExitStack

import concourse.bass as bass
from concourse import mybir

ALU = mybir.AluOpType
ACT = mybir.ActivationFunctionType
AX = mybir.AxisListType
F32 = mybir.dt.float32
I32 = mybir.dt.int32

P = 128
TB = 4
GT = 4
EPS_LN = 1e-5
EPS_RMS = 1e-6
NEWTON = 3
ROOT_OPS = 2 + 4 * NEWTON
NORM_OPS = 4 + ROOT_OPS + 1

STEPS = 64
O_AT = 0
L3_AT = 17
FL_AT = 21
F_AT = 21
ROUTE_T_AT = 24
E0_AT = 12
E1_AT = 20
E2_AT = 29
E3_AT = 31
X_AT = 36
XP_LAG = 5
BC_AT = 57
BCT_AT = 58
DT_AT = 8
DT_AT3 = 60
W_O, W_F, W_I = 0, 16, 24


def z_tiles(s):
    if 52 <= s < 56:
        return [s - 52]
    if 56 <= s < 60:
        return [4 + 2 * (s - 56), 5 + 2 * (s - 56)]
    if 60 <= s < 64:
        return [12 + s - 60]
    return []


def dt_tiles(s):
    g, n = s // 16, s % 16
    if g < 3:
        return [n - DT_AT] if DT_AT <= n < DT_AT + GT else []
    return [2 * (s - DT_AT3), 2 * (s - DT_AT3) + 1] if DT_AT3 <= s < DT_AT3 + 2 else []


def ge(eng, sem, value):
    if isinstance(value, int) and value <= 0:
        return
    eng.wait_ge(sem, value)


class It:

    def __init__(self, b, nb):
        known = isinstance(b, int)
        self.b = b
        self.scan = not known or 0 <= b < nb
        self.behind = not known or 1 <= b <= nb
        self.ahead = not known or b + 1 < nb
        self.scan_before = not known or 0 <= b - 1 < nb
        self.ahead_before = not known or (b >= 0 and b < nb)
        if known:
            self.w_base = [0, 8][b + 1] if b <= 0 else 16 + 14 * min(b - 1, nb - 2) + (6 if b == nb else 0)
        else:
            self.w_base = 16 + 14 * (b - 1)
        self.w_first = W_I if known and b <= 0 else 0

    def w_count(self, pos):
        return self.w_base + (pos - self.w_first) // 4


def build(nc, ids, ein, wout, probs_col, w_in, conv_w, conv_b, wx, dtw, dt_bias, a_log, d_par, ln_w,
          w_o, w_f, ag, bt, gate_b, out):
    NB, L, H = out.shape
    DT = conv_w.shape[1]
    KH = H // P
    R = dtw.shape[0]
    N = a_log.shape[2]
    E = wx.shape[2]
    LR = bt.shape[0] - 1
    NR = ag.shape[2] - LR
    GROUPS = DT // GT
    assert GROUPS * N == STEPS and L == TB * P

    h_dram = nc.dram_tensor("h_spill", (NB, L, H), F32, kind="Internal").ap()
    xc_dram = nc.dram_tensor("xc_spill", (NB, DT, P, L), F32, kind="Internal").ap()
    sz_dram = nc.dram_tensor("silu_z_spill", (NB, DT, P, L), F32, kind="Internal").ap()
    y_dram = nc.dram_tensor("y_spill", (NB, DT, P, L), F32, kind="Internal").ap()
    b_dram = nc.dram_tensor("b_rows", (NB, 1, N * L), F32, kind="Internal").ap()

    with ExitStack() as ctx:
        def sb(name, shape, dt=F32):
            return ctx.enter_context(nc.sbuf_tensor(name, shape, dt))

        def psum(name, shape):
            return ctx.enter_context(nc.psum_tensor(name, shape, F32))

        def sem(name):
            return ctx.enter_context(nc.semaphore(name))

        w_ring = sb("w_ring", [P, 4, 1024])
        hnT = sb("hnT", [P, KH, L])
        res = sb("res", [P, TB, H])
        res_flat = res[:, :, :].rearrange("p a b -> p (a b)")
        cz = res_flat[:, 0:2048].rearrange("p (s t) -> p s t", s=4)
        xin = res_flat[:, 2048:2048 + 2 * 516].rearrange("p (s t) -> p s t", s=2)
        q_reg = sb("q_reg", [P, 2048])
        y_in = q_reg[:, :].rearrange("p (s i t) -> p s i t", s=2, i=2)
        lowT = q_reg[:, 0:1024].rearrange("p (b k t) -> p b k t", b=4, k=2)
        hn = q_reg[:, 1024:2048]
        h_row = sb("h_row", [P, H])
        low = sb("low", [P, TB, 256])
        idx = sb("idx", [P, TB], I32)
        wout_sb = sb("wout_sb", [P, 2, H])
        wx_sb = sb("wx_sb", [P, DT, E])
        dtw_sb = sb("dtw_sb", [R, L])
        ag_sb = sb("ag_sb", [P, KH, LR + NR])
        bt_sb = sb("bt_sb", [LR + 1, H])
        dt_sb = sb("dt_sb", [P, 2, GT, L])
        u_sb = sb("u_sb", [P, 2, GT, L])
        sp_tmp = sb("sp_tmp", [P, 2, L])
        xcg = sb("xcg", [P, GT, L])
        szg = sb("szg", [P, GT, L])
        dA = sb("dA", [P, 2, GT, L])
        dBx = sb("dBx", [P, GT, L])
        h_sb = sb("h_sb", [P, 2, GT, L])
        b_row = sb("b_row", [P, 4, L])
        y_acc = sb("y_acc", [P, TB, GT * P])
        dtB = sb("dtB", [R + N, L])
        xmT = sb("xmT", [LR + 1, L])
        xm = sb("xm", [P, TB, LR + 1])
        bcn = sb("bcn", [P, TB, E])
        c_now = sb("c_now", [P, TB, N])
        a_sb = sb("a_sb", [P, DT, N])
        ident = sb("ident", [P, P])
        zero_sb = sb("zero_sb", [P, P])
        cw_sb = sb("cw_sb", [P, DT, 4])
        cb_sb = sb("cb_sb", [P, DT])
        dtb_sb = sb("dtb_sb", [P, DT])
        d_sb = sb("d_sb", [P, DT])
        lnw_sb = sb("lnw_sb", [P, E])
        gb_sb = sb("gb_sb", [P, TB, NR])
        pc_sb = sb("pc_sb", [P, 2])
        stats = sb("stats", [P, 2, 6])
        mv = sb("mv", [P, 2])
        rstd = sb("rstd", [P, 1])
        rms = sb("rms", [P, 6, TB])
        rtmp = sb("rtmp", [P, 3 * TB])
        route = sb("route", [P, 3, TB, NR])
        route1 = sb("route1", [P, 4, TB])

        fill_ps = psum("fill_ps", [P, 4, L])
        x_ps = psum("x_ps", [P, L])
        m_ps = psum("m_ps", [P, L])
        hT_ps = psum("hT_ps", [P, 2, L])

        w_loaded = [sem(f"w_loaded{j}") for j in range(4)]
        w_used = [sem(f"w_used{j}") for j in range(4)]
        y_loaded = [sem(f"y_loaded{j}") for j in range(2)]
        y_stored = [sem(f"y_stored{j}") for j in range(2)]
        b_loaded = [sem(f"b_loaded{j}") for j in range(4)]
        u_loaded = [sem(f"u_loaded{j}") for j in range(2)]
        cz_stored = [sem(f"cz_stored{j}") for j in range(4)]
        low_loaded = [sem(f"low_loaded{j}") for j in range(TB)]
        xcg_loaded, szg_loaded, dtw_loaded, idx_loaded, res_loaded = (
            sem(n) for n in ("xcg_loaded", "szg_loaded", "dtw_loaded", "idx_loaded", "res_loaded"))
        h_stored, out_stored, b_stored, consts = (sem(n) for n in ("h_stored", "out_stored", "b_stored", "consts"))
        hT_ready, back_mm, dt_mm, o_step, o_mm, l3_mm, fl_mm, rt_mm, f_mm, e1_mm, e2_mm, e3_mm, i_mm, xp_mm, bct_mm = (
            sem(n) for n in ("hT_ready", "back_mm", "dt_mm", "o_step", "o_mm", "l3_mm", "fl_mm", "rt_mm", "f_mm",
                             "e1_mm", "e2_mm", "e3_mm", "i_mm", "xp_mm", "bct_mm"))
        scan_done, stt_done, gate_done, o_added, f_added, conv_done, e2_norm, h2n_done, shifted, routed, bc_done, c_copied = (
            sem(n) for n in ("scan_done", "stt_done", "gate_done", "o_added", "f_added", "conv_done", "e2_norm",
                             "h2n_done", "shifted", "routed", "bc_done", "c_copied"))
        e_chain, l_chain, conv_chain, sh_chain, rt_chain, bc_chain = (
            sem(n) for n in ("e_chain", "l_chain", "conv_chain", "sh_chain", "rt_chain", "bc_chain"))
        setup_v, setup_a, setup_p = sem("setup_v"), sem("setup_a"), sem("setup_p")
        exp_done, e1_evac, e2_copied, e3_evac, l3_evac, i_evac, silu_done, dt_evac, sp_chain, sp_done, exp_scores, rt_evac, bct_evac = (
            sem(n) for n in ("exp_done", "e1_evac", "e2_copied", "e3_evac", "l3_evac", "i_evac", "silu_done",
                             "dt_evac", "sp_chain", "sp_done", "exp_scores", "rt_evac", "bct_evac"))
        mul_done, dtu_chain, dtu_done, yg_done = (sem(n) for n in ("mul_done", "dtu_chain", "dtu_done", "yg_done"))

        NCONST = 12
        block = ctx.enter_context(nc.Block())

        def run(eng, step, first, last, nb=NB):
            for b in (-1, 0):
                for s in range(STEPS):
                    step(It(b, nb), s)
            with eng.Fori(1, nb - 1) as b:
                for s in range(STEPS):
                    step(It(b, nb), s)
            for b in (nb - 1, nb):
                for s in range(STEPS if b < nb else 34):
                    step(It(b, nb), s)

        @block.sync
        def _(sp):
            def load_w(it, pos, src):
                j, n = pos % 4, it.w_count(pos)
                ge(sp, w_used[j], n)
                sp.dma_start(w_ring[:, j, :], src).then_inc(w_loaded[j], 16)

            def step(it, s):
                bb = it.b - 1
                if it.behind and s < 16:
                    load_w(it, W_O + s, w_o[s])
                    if s == 0:
                        if it.ahead_before:
                            ge(sp, e3_mm, 4 * (it.b + 1))
                        else:
                            ge(sp, o_mm, 2 * bb)
                    kp, p = s % 8, s % 2
                    if s >= 2:
                        sp.wait_ge(o_step, 16 * bb + s - 1)
                    ge(sp, y_stored[p], 16 * (4 * bb + kp // 2 + 1))
                    sp.dma_start(y_in[:, p, :, :], y_dram[bass.ds(bb, 1), 2 * kp:2 * kp + 2, :, :]
                                 .rearrange("o i p t -> p (o i) t")).then_inc(y_loaded[p], 16)
                if it.behind and F_AT <= s < F_AT + 8:
                    load_w(it, W_F + s - F_AT, w_f[s - F_AT])
                if it.ahead and X_AT <= s < X_AT + 16:
                    load_w(it, W_I + s - X_AT, w_in[s - X_AT])
                if it.ahead:
                    for z in z_tiles(s):
                        load_w(it, W_I + 16 + z, w_in[16 + z])

            for dst, src in ((a_sb, a_log), (cw_sb, conv_w), (cb_sb, conv_b), (dtb_sb, dt_bias), (d_sb, d_par),
                             (lnw_sb, ln_w), (gb_sb, gate_b), (pc_sb, probs_col), (wout_sb, wout), (wx_sb, wx),
                             (ag_sb, ag), (bt_sb, bt)):
                sp.dma_start(dst[:], src).then_inc(consts, 16)
            run(sp, step, 0, 0)

        @block.gpsimd
        def _(pool):
            nc.gpsimd.memset(zero_sb[:], 0.0).then_inc(setup_p, 1)
            pool.wait_ge(setup_p, 1)
            nc.gpsimd.affine_select(out=ident[:, :], in_=zero_sb[:, :], compare_op=ALU.not_equal, fill=1.0, base=0,
                                    pattern=[[-1, P]], channel_multiplier=1).then_inc(setup_p, 1)
            nc.gpsimd.memset(xm[:], 1.0).then_inc(setup_p, 1)

            def gather(it, tb):
                bb = it.b + 1
                if tb == 0:
                    pool.wait_ge(idx_loaded, 16 * (bb + 1))
                ge(pool, e1_mm, 4 * bb)
                pool.nop(nofuse=True)
                nc.gpsimd.indirect_dma_start(
                    out=low[:, tb, :], out_offset=None, in_=ein,
                    in_offset=bass.IndirectOffsetOnAxis(ap=idx[:, tb:tb + 1], axis=0)).then_inc(low_loaded[tb], 16)

            def delta(gn, p, i):
                base = 2 * (4 * gn + i)
                pool.wait_ge(dt_evac, 4 * gn + i + 1)
                pool.wait_ge(sp_done, 4 * gn + i + 1)
                pool.nop(nofuse=True)
                nc.gpsimd.tensor_scalar(dt_sb[:, p, i, :], dt_sb[:, p, i, :], 0.0, None, ALU.max).then_inc(dtu_chain, 1)
                pool.wait_ge(dtu_chain, base + 1)
                nc.gpsimd.tensor_tensor(dt_sb[:, p, i, :], dt_sb[:, p, i, :], sp_tmp[:, i % 2, :], ALU.add) \
                    .then_inc(dtu_chain, 1)
                pool.wait_ge(dtu_chain, base + 2)
                if i == 0:
                    pool.wait_ge(u_loaded[p], 8 * (gn - p) + 16)
                nc.gpsimd.tensor_tensor(u_sb[:, p, i, :], u_sb[:, p, i, :], dt_sb[:, p, i, :], ALU.mult) \
                    .then_inc(dtu_done, 1)

            def step(it, s):
                S, g, n = STEPS * it.b + s, s // 16, s % 16
                G = GROUPS * it.b + g
                if it.scan:
                    pool.wait_ge(b_loaded[s % 4], 16 * (16 * it.b + s // 4 + 1))
                    for i in range(GT):
                        if n == 0:
                            pool.wait_ge(dtu_done, 4 * G + i + 1)
                        ge(pool, scan_done, 4 * (S - 1) + i + 1)
                        nc.gpsimd.tensor_tensor(dBx[:, i, :], u_sb[:, g % 2, i, :], b_row[:, s % 4, :], ALU.mult) \
                            .then_inc(mul_done, 1)
                if n in (2, 3) and (it.scan if g else it.scan_before):
                    for i in (2 * (n - 2), 2 * (n - 2) + 1):
                        pool.wait_ge(gate_done, 4 * (G - 1) + i + 1)
                        if i == 0:
                            pool.wait_ge(szg_loaded, 16 * G)
                        nc.gpsimd.tensor_tensor(szg[:, i, :], szg[:, i, :], xcg[:, i, :], ALU.mult).then_inc(yg_done, 1)
                t = s - (2 if g == 3 and n >= 12 else 3)
                if t >= 0 and (it.scan if t // 16 < 3 else it.ahead):
                    for i in dt_tiles(t):
                        delta(GROUPS * it.b + t // 16 + 1, (t // 16 + 1) % 2, i)
                if it.ahead and E0_AT <= s < E0_AT + 2 * TB and (s - E0_AT) % 2 == 0:
                    gather(it, (s - E0_AT) // 2)

            run(pool, step, 0, 0)

        @block.tensor
        def _(pe):
            pe.wait_ge(consts, 16 * NCONST)
            pe.wait_ge(setup_p, 3)
            pe.wait_ge(setup_v, 3)

            def states_transposed(it, s, tb):
                S = STEPS * it.b + s
                if tb == 0:
                    pe.wait_ge(scan_done, 4 * S + 4)
                ge(pe, stt_done, 4 * S + tb - 1)
                for i in range(GT):
                    mm = nc.tensor.transpose(hT_ps[:, tb % 2, i * P:(i + 1) * P],
                                             h_sb[:, s % 2, i, tb * P:(tb + 1) * P], ident[:, :])
                mm.then_inc(hT_ready, 1)

            def y_back(it, s):
                g, G = s // 16, GROUPS * it.b + s // 16
                for i in range(GT):
                    if i == 0:
                        pe.wait_ge(stt_done, 4 * (STEPS * it.b + s))
                        if it.scan and g or it.ahead_before:
                            ge(pe, dt_evac, 4 * G + 4)
                        else:
                            ge(pe, dt_evac, 4 * G)
                        if g == 2 and it.ahead:
                            pe.wait_ge(e3_evac, 4 * (it.b + 1) + s - E3_AT + 1)
                    else:
                        pe.wait_ge(gate_done, 4 * (G - 1) + i)
                    for tb in range(TB):
                        mm = nc.tensor.transpose(m_ps[:, tb * P:(tb + 1) * P], y_acc[:, tb, i * P:(i + 1) * P], ident[:, :])
                    mm.then_inc(back_mm, 1)

            def dt_raw(it, s, i):
                g = s // 16
                gn = GROUPS * it.b + g + 1
                bank = x_ps if g == 3 and i % 2 else m_ps
                if i == 0:
                    pe.wait_ge(dtw_loaded, 16 * (gn + 1))
                    if it.scan:
                        ge(pe, gate_done, 4 * (gn - 1))
                    if g == 1 and it.ahead:
                        pe.wait_ge(e1_evac, 4 * (it.b + 1) + 4)
                    if g == 2 and it.ahead:
                        pe.wait_ge(e3_evac, 4 * (it.b + 1) + 4)
                    if g == 3:
                        pe.wait_ge(bct_evac, it.b + 2)
                if g == 3:
                    ge(pe, dt_evac, 4 * gn + i - 1)
                else:
                    ge(pe, dt_evac, 4 * gn + i)
                nc.tensor.matmul(bank[:, :], dtw_sb[:, i * P:(i + 1) * P], dtB[0:R, :], start=True, stop=True) \
                    .then_inc(dt_mm, 1)

            def out_rows(it, s, m):
                bb, half, kp, p = it.b - 1, s // 8, s % 8, s % 2
                i, tb = m // 4, m % 4
                if m == 0:
                    pe.wait_ge(w_loaded[s % 4], 16 * (it.w_count(W_O + s) + 1))
                    pe.wait_ge(y_loaded[p], 16 * (8 * bb + s // 2 + 1))
                if kp == 0 and i == 0:
                    if half == 0 and tb == 0 and it.ahead_before:
                        pe.wait_ge(i_evac, 32 * (it.b + 1))
                    elif half == 1:
                        pe.wait_ge(o_added, 8 * bb + tb + 1)
                mm = nc.tensor.matmul(fill_ps[:, tb, :], y_in[:, p, i, tb * P:(tb + 1) * P],
                                      w_ring[:, s % 4, i * L:(i + 1) * L], start=(kp == 0 and i == 0),
                                      stop=(kp == 7 and i == 1))
                if m == 7:
                    mm.then_inc(w_used[s % 4], 1)
                    pe.wait_ge(w_used[s % 4], it.w_count(W_O + s) + 1)
                    pe.sem_inc(o_step, 1)
                    if kp == 7:
                        pe.sem_inc(o_mm, 1)

            def dense_rows(it, s, m):
                bb, t = it.b - 1, s - F_AT
                half, kp, i, tb = t // 4, t % 4, m // 4, m % 4
                if m == 0:
                    pe.wait_ge(w_loaded[t % 4], 16 * (it.w_count(W_F + t) + 1))
                if half == 1 and kp == 0 and i == 0:
                    pe.wait_ge(f_added, 8 * bb + tb + 1)
                mm = nc.tensor.matmul(fill_ps[:, tb, :], hnT[:, 2 * kp + i, tb * P:(tb + 1) * P],
                                      w_ring[:, t % 4, i * L:(i + 1) * L], start=(kp == 0 and i == 0), stop=False)
                if m == 7:
                    mm.then_inc(w_used[t % 4], 1)

            def low_rank_rows(it, half):
                bb = it.b - 1
                pe.wait_ge(rt_evac, bb + 1)
                for tb in range(TB):
                    mm = nc.tensor.matmul(fill_ps[:, tb, :], xmT[:, tb * P:(tb + 1) * P], bt_sb[:, half * L:(half + 1) * L],
                                          start=False, stop=True)
                mm.then_inc(f_mm, 1)

            def in_rows(it, e, part, parts):
                bb, j = it.b + 1, e % 4
                per = KH // parts
                if part == 0:
                    pe.wait_ge(w_loaded[j], 16 * (it.w_count(W_I + e) + 1))
                    if e < 4:
                        pe.wait_ge(e2_norm, 4 * bb + 4)
                        pe.wait_ge(e2_copied, 4 * bb + 4)
                    else:
                        pe.wait_ge(i_evac, 32 * bb + e - 3)
                    if e == 0:
                        pe.wait_ge(e3_evac, 4 * bb + 4)
                for k in range(part * per, (part + 1) * per):
                    mm = nc.tensor.matmul(fill_ps[:, j, :], w_ring[:, j, k * P:(k + 1) * P], hnT[:, k, :],
                                          start=(k == 0), stop=(k == KH - 1))
                if part == parts - 1:
                    mm.then_inc(i_mm, 1)
                    pe.wait_ge(i_mm, 32 * bb + e + 1)
                    pe.sem_inc(w_used[j], 1)

            def embed_rows(it, tb, part):
                bb, half = it.b + 1, part // 2
                if part == 0:
                    if tb < 2:
                        if it.behind:
                            pe.wait_ge(f_added, 8 * (it.b - 1) + 8)
                        elif it.ahead_before:
                            pe.wait_ge(i_evac, 32 * (it.b + 1))
                    else:
                        pe.wait_ge(e2_norm, 4 * bb + tb - 1)
                        pe.wait_ge(e2_copied, 4 * bb + tb - 1)
                    pe.wait_ge(e1_evac, 4 * bb + tb + 1)
                if part % 2 == 0:
                    for k in range(2):
                        mm = nc.tensor.matmul(fill_ps[:, 2 * (tb % 2) + half, :], lowT[:, tb, k, :],
                                              wout_sb[:, k, half * L:(half + 1) * L], start=(k == 0), stop=(k == 1))
                    if half == 1:
                        mm.then_inc(e2_mm, 1)

            def fill(it, s, part):
                if it.behind and s < 16:
                    for m in (2 * part, 2 * part + 1):
                        out_rows(it, s, m)
                if it.behind and F_AT <= s < F_AT + 8:
                    for m in (2 * part, 2 * part + 1):
                        dense_rows(it, s, m)
                if it.ahead and E2_AT <= s < E2_AT + TB:
                    embed_rows(it, s - E2_AT, part)
                if it.ahead and X_AT <= s < X_AT + 16:
                    in_rows(it, s - X_AT, part, 4)
                if it.ahead:
                    zs = z_tiles(s)
                    if len(zs) == 1:
                        in_rows(it, 16 + zs[0], part, 4)
                    elif zs:
                        in_rows(it, 16 + zs[part // 2], part % 2, 2)

            def before(it, s):
                bb = it.b - 1
                if it.behind and L3_AT <= s < L3_AT + TB:
                    tb = s - L3_AT
                    pe.wait_ge(h2n_done, 4 * bb + tb + 1)
                    if tb < 2:
                        pe.wait_ge(o_added, 8 * bb + 8)
                    else:
                        pe.wait_ge(l3_evac, 4 * bb + tb - 1)
                    for k in range(KH):
                        mm = nc.tensor.transpose(fill_ps[:, 2 * (tb % 2) + k // 4, (k % 4) * P:(k % 4 + 1) * P],
                                                 h_row[:, k * P:(k + 1) * P], ident[:, :])
                    mm.then_inc(l3_mm, 1)
                if it.behind and s == FL_AT:
                    pe.wait_ge(l3_evac, 4 * bb + 4)
                    if it.ahead_before:
                        pe.wait_ge(dt_evac, 16 * it.b + 4)
                    for tb in range(TB):
                        for k in range(KH):
                            mm = nc.tensor.matmul(x_ps[:, tb * (LR + NR):(tb + 1) * (LR + NR)],
                                                  hnT[:, k, tb * P:(tb + 1) * P], ag_sb[:, k, :],
                                                  start=(k == 0), stop=(k == KH - 1))
                    mm.then_inc(fl_mm, 1)
                if it.behind and s == ROUTE_T_AT:
                    pe.wait_ge(routed, bb + 1)
                    for tb in range(TB):
                        mm = nc.tensor.transpose(x_ps[0:LR + 1, tb * P:(tb + 1) * P], xm[:, tb, :], ident[:, :])
                    mm.then_inc(rt_mm, 1)
                bb = it.b + 1
                if it.ahead and E1_AT <= s < E1_AT + TB:
                    tb = s - E1_AT
                    if tb == 0:
                        if it.scan:
                            pe.wait_ge(gate_done, 16 * it.b + 4)
                    else:
                        pe.wait_ge(e1_evac, 4 * bb + tb)
                    pe.wait_ge(low_loaded[tb], 16 * (bb + 1))
                    for k in range(2):
                        mm = nc.tensor.transpose(m_ps[:, k * P:(k + 1) * P], low[:, tb, k * P:(k + 1) * P], ident[:, :])
                    mm.then_inc(e1_mm, 1)
                if it.ahead and E3_AT <= s < E3_AT + TB:
                    tb = s - E3_AT
                    pe.wait_ge(e2_norm, 4 * bb + tb + 1)
                    if tb == 0:
                        if it.scan:
                            pe.wait_ge(dt_evac, 16 * it.b + 12)
                        else:
                            pe.wait_ge(e1_evac, 4 * bb + 4)
                        if it.behind:
                            pe.wait_ge(rt_evac, it.b)
                    else:
                        pe.wait_ge(e3_evac, 4 * bb + tb)
                    if s == 33 and it.scan:
                        pe.wait_ge(gate_done, 16 * it.b + 8)
                    for k in range(KH):
                        mm = nc.tensor.transpose((x_ps if k < 4 else m_ps)[:, (k % 4) * P:(k % 4 + 1) * P],
                                                 hn[:, k * P:(k + 1) * P], ident[:, :])
                    mm.then_inc(e3_mm, 1)
                e = s - X_AT - XP_LAG
                if it.ahead and 0 <= e < 16:
                    pe.wait_ge(silu_done, 16 * bb + e + 1)
                    for tb in range(TB):
                        mm = nc.tensor.matmul(x_ps[:, tb * E:(tb + 1) * E], cz[:, e % 4, tb * P:(tb + 1) * P],
                                              wx_sb[:, e, :], start=(e == 0 and tb == 0), stop=(e == 15),
                                              skip_group_check=True)
                    mm.then_inc(xp_mm, 1)
                if it.ahead and s == BCT_AT:
                    pe.wait_ge(bc_done, bb + 1)
                    if it.scan:
                        pe.wait_ge(gate_done, 16 * it.b + 12)
                    for tb in range(TB):
                        mm = nc.tensor.transpose(m_ps[0:R + N, tb * P:(tb + 1) * P], bcn[:, tb, 0:R + N], ident[:, :])
                    mm.then_inc(bct_mm, 1)
                if it.scan if s // 16 < 3 else it.ahead:
                    for i in dt_tiles(s):
                        dt_raw(it, s, i)

            def step(it, s):
                before(it, s)
                for tb in range(TB):
                    if it.scan:
                        states_transposed(it, s, tb)
                    fill(it, s, tb)
                    if tb == 1 and s % 16 == 0 and (it.scan if s else it.scan_before):
                        y_back(it, s)
                if it.behind and s in (F_AT + 3, F_AT + 7):
                    low_rank_rows(it, (s - F_AT) // 4)

            run(pe, step, 0, 0)

        @block.vector
        def _(dve):
            dve.wait_ge(consts, 16 * NCONST)
            dve.wait_ge(setup_a, 1)
            nc.vector.tensor_scalar(a_sb[:], a_sb[:], -1.0, None, ALU.mult).then_inc(setup_v, 1)
            for k in range(2):
                nc.vector.tensor_scalar(wout_sb[:, k, :], wout_sb[:, k, :], pc_sb[:, k:k + 1], None, ALU.mult) \
                    .then_inc(setup_v, 1)

            def linked(chain, at, ins):
                ins.then_inc(chain, 1)
                dve.wait_ge(chain, at)

            def accumulate(it, s, tb):
                S, n = STEPS * it.b + s - 1, (s - 1) % 16
                dve.wait_ge(hT_ready, 4 * S + tb + 1)
                if n == 0:
                    nc.vector.tensor_scalar(y_acc[:, tb, :], hT_ps[:, tb % 2, :], c_now[:, tb, n:n + 1], None, ALU.mult) \
                        .then_inc(stt_done, 1)
                else:
                    dve.wait_ge(stt_done, 4 * (S - 1) + tb + 1)
                    nc.vector.scalar_tensor_tensor(out=y_acc[:, tb, :], in0=hT_ps[:, tb % 2, :],
                                                   scalar=c_now[:, tb, n:n + 1], in1=y_acc[:, tb, :],
                                                   op0=ALU.mult, op1=ALU.add).then_inc(stt_done, 1)

            def gate(it, s, i):
                G = GROUPS * it.b + s // 16 - 1
                gp = (s // 16 - 1) % GROUPS
                dve.wait_ge(back_mm, 4 * G + i + 1)
                if i == 0:
                    dve.wait_ge(xcg_loaded, 16 * (G + 1))
                nc.vector.scalar_tensor_tensor(out=xcg[:, i, :], in0=xcg[:, i, :], scalar=d_sb[:, 4 * gp + i:4 * gp + i + 1],
                                               in1=m_ps[:, :], op0=ALU.mult, op1=ALU.add).then_inc(gate_done, 1)

            def inverse_root(v, y, tmp, chain, at):
                linked(chain, at + 1, nc.vector.tensor_scalar(tmp.bitcast(I32), v.bitcast(I32), 1, None,
                                                              ALU.arith_shift_right))
                linked(chain, at + 2, nc.vector.tensor_scalar(y.bitcast(I32), tmp.bitcast(I32), -1.0, float(0x5F3759DF),
                                                              ALU.mult, ALU.add))
                for k in range(NEWTON):
                    linked(chain, at + 4 * k + 3, nc.vector.tensor_tensor(tmp, y, y, ALU.mult))
                    linked(chain, at + 4 * k + 4, nc.vector.tensor_tensor(tmp, tmp, v, ALU.mult))
                    linked(chain, at + 4 * k + 5, nc.vector.tensor_scalar(tmp, tmp, -0.5, 1.5, ALU.mult, ALU.add))
                    linked(chain, at + 4 * k + 6, nc.vector.tensor_tensor(y, y, tmp, ALU.mult))

            def layernorm(src0, src1, dst, chain, base, last):
                linked(chain, base + 1, nc.vector.bn_stats(stats[:, 0, :], src0))
                linked(chain, base + 2, nc.vector.bn_stats(stats[:, 1, :], src1))
                dve.nop(nofuse=True)
                linked(chain, base + 3, nc.vector.bn_aggr(mv[:, :], stats[:, :, :].rearrange("p a b -> p (a b)")))
                linked(chain, base + 4, nc.vector.tensor_scalar(mv[:, 1:2], mv[:, 1:2], EPS_LN, None, ALU.add))
                inverse_root(mv[:, 1:2], rstd[:, :], rtmp[:, 0:1], chain, base + 4)
                nc.vector.tensor_scalar(dst[:, 0:L], src0, mv[:, 0:1], rstd[:, 0:1], ALU.subtract, ALU.mult) \
                    .then_inc(chain, 1)
                nc.vector.tensor_scalar(dst[:, L:2 * L], src1, mv[:, 0:1], rstd[:, 0:1], ALU.subtract, ALU.mult) \
                    .then_inc(last, 1)
                dve.wait_ge(chain, base + NORM_OPS)

            def embed_norm(it, tb):
                bb = it.b + 1
                dve.wait_ge(e2_mm, 4 * bb + tb + 1)
                if tb == 0 and it.behind:
                    dve.wait_ge(o_mm, 2 * it.b)
                ge(dve, e3_mm, 4 * bb + tb)
                ge(dve, e2_norm, 4 * bb + tb)
                bank = 2 * (tb % 2)
                layernorm(fill_ps[:, bank, :], fill_ps[:, bank + 1, :], hn, e_chain, NORM_OPS * (4 * bb + tb), e2_norm)

            def second_norm(it, tb):
                bb = it.b - 1
                if tb:
                    dve.wait_ge(l3_mm, 4 * bb + tb)
                elif it.ahead_before:
                    dve.wait_ge(i_mm, 32 * (it.b + 1))
                else:
                    dve.wait_ge(l3_mm, 4 * bb)
                if tb == 0:
                    dve.wait_ge(o_added, 8 * bb + 8)
                    dve.wait_ge(h_stored, 64 * it.b if not it.ahead_before else 64 * (it.b + 1))
                layernorm(res[:, tb, 0:L], res[:, tb, L:2 * L], h_row, l_chain, NORM_OPS * (4 * bb + tb), h2n_done)

            def add_rows(it, half, done, mm):
                bb = it.b - 1
                dve.wait_ge(mm, 2 * bb + half + 1)
                if half == 0:
                    dve.wait_ge(res_loaded, 16 * (bb + 1))
                for tb in range(TB):
                    nc.vector.tensor_tensor(res[:, tb, half * L:(half + 1) * L], res[:, tb, half * L:(half + 1) * L],
                                            fill_ps[:, tb, :], ALU.add).then_inc(done, 1)

            def conv(it, e):
                bb, base = it.b + 1, 4 * (16 * (it.b + 1) + e)
                c = cz[:, e % 4, :]
                x = xin[:, e % 2, :]
                if e < 4:
                    ge(dve, cz_stored[e], 16 * 8 * bb)
                else:
                    dve.wait_ge(cz_stored[e % 4], 16 * (8 * bb + e // 4))
                    dve.wait_ge(xp_mm, 16 * bb + e - 3)
                nc.vector.memset(x[:, 0:3], 0.0).then_inc(conv_chain, 1)
                dve.wait_ge(conv_chain, base + 1)
                dve.wait_ge(i_evac, 32 * bb + e + 1)
                linked(conv_chain, base + 2, nc.vector.tensor_scalar(c, x[:, 0:L], cw_sb[:, e, 0:1], cb_sb[:, e:e + 1],
                                                                     ALU.mult, ALU.add))
                for k in (1, 2):
                    linked(conv_chain, base + 2 + k, nc.vector.scalar_tensor_tensor(
                        out=c, in0=x[:, k:k + L], scalar=cw_sb[:, e, k:k + 1], in1=c, op0=ALU.mult, op1=ALU.add))
                nc.vector.scalar_tensor_tensor(out=c, in0=x[:, 3:3 + L], scalar=cw_sb[:, e, 3:4], in1=c,
                                               op0=ALU.mult, op1=ALU.add).then_inc(conv_done, 1)

            def scores(it):
                bb, base = it.b - 1, 2 * (it.b - 1)
                x = x_ps[:, 0:TB * (LR + NR)].rearrange("p (b c) -> p b c", b=TB)
                dve.wait_ge(fl_mm, bb + 1)
                linked(sh_chain, base + 1, nc.vector.tensor_tensor(route[:, 0, :, :], x[:, :, LR:LR + NR], gb_sb[:, :, :],
                                                                   ALU.add))
                linked(sh_chain, base + 2, nc.vector.tensor_reduce(route1[:, 0, :], route[:, 0, :, :], AX.X, ALU.max))
                nc.vector.tensor_tensor(route[:, 0, :, :], route[:, 0, :, :],
                                        route1[:, 0, :].unsqueeze(2).to_broadcast([P, TB, NR]), ALU.subtract) \
                    .then_inc(shifted, 1)

            def choose(it):
                bb, base = it.b - 1, 10 * (it.b - 1)
                x = x_ps[:, 0:TB * (LR + NR)].rearrange("p (b c) -> p b c", b=TB)
                ex, pr, mk = route[:, 1, :, :], route[:, 0, :, :], route[:, 2, :, :]
                total, top, inv = route1[:, 1, :], route1[:, 2, :], route1[:, 3, :]
                at = [base]

                def then(ins):
                    at[0] += 1
                    linked(rt_chain, at[0], ins)

                dve.wait_ge(exp_scores, bb + 1)
                then(nc.vector.tensor_reduce(total, ex, AX.X, ALU.add))
                then(nc.vector.reciprocal(inv, total))
                then(nc.vector.tensor_tensor(pr, ex, inv.unsqueeze(2).to_broadcast([P, TB, NR]), ALU.mult))
                then(nc.vector.tensor_reduce(top, pr, AX.X, ALU.max))
                then(nc.vector.reciprocal(inv, top))
                then(nc.vector.tensor_tensor(mk[:, :, 0], top, inv, ALU.mult))
                then(nc.vector.tensor_tensor(ex, pr, top.unsqueeze(2).to_broadcast([P, TB, NR]), ALU.is_lt))
                for r in range(1, NR):
                    then(nc.vector.tensor_tensor(mk[:, :, r], mk[:, :, r - 1], ex[:, :, r - 1], ALU.mult))
                if it.ahead_before:
                    dve.wait_ge(i_mm, 32 * (it.b + 1))
                else:
                    dve.wait_ge(rt_mm, bb)
                lo = 0
                for r, hi in enumerate((8, 16, 32, 64)):
                    ins = nc.vector.tensor_tensor(xm[:, :, lo:hi], x[:, :, lo:hi],
                                                  mk[:, :, r:r + 1].to_broadcast([P, TB, hi - lo]), ALU.mult)
                    lo = hi
                ins.then_inc(routed, 1)

            def project_norms(it):
                bb, base = it.b + 1, (5 + ROOT_OPS) * (it.b + 1)
                x = x_ps[:, 0:TB * E].rearrange("p (b c) -> p b c", b=TB)
                sq = h_row[:, 0:TB * E].rearrange("p (b c) -> p b c", b=TB)
                dve.wait_ge(xp_mm, 16 * bb + 16)
                dve.wait_ge(h_stored, 64 * (bb + 1))
                linked(bc_chain, base + 1, nc.vector.tensor_copy(bcn[:, :, :], x))
                linked(bc_chain, base + 2, nc.vector.tensor_tensor(sq, bcn[:, :, :], bcn[:, :, :], ALU.mult))
                cuts = ((0, R), (R, R + N), (R + N, E))
                for k, (lo, hi) in enumerate(cuts):
                    ins = nc.vector.tensor_reduce(rms[:, k, :], sq[:, :, lo:hi], AX.X, ALU.add)
                linked(bc_chain, base + 3, ins)
                for k, (lo, hi) in enumerate(cuts):
                    ins = nc.vector.tensor_scalar(rms[:, k, :], rms[:, k, :], 1.0 / (hi - lo), EPS_RMS, ALU.mult, ALU.add)
                linked(bc_chain, base + 4, ins)
                inverse_root(rms[:, 0:3, :], rms[:, 3:6, :], rtmp[:, :].rearrange("p (a b) -> p a b", a=3), bc_chain, base + 4)
                for k, (lo, hi) in enumerate(cuts):
                    ins = nc.vector.tensor_tensor(sq[:, :, lo:hi], bcn[:, :, lo:hi],
                                                  rms[:, 3 + k, :].unsqueeze(2).to_broadcast([P, TB, hi - lo]), ALU.mult)
                linked(bc_chain, base + 5 + ROOT_OPS, ins)
                nc.vector.tensor_tensor(bcn[:, :, :], sq, lnw_sb[:, :].unsqueeze(1).to_broadcast([P, TB, E]), ALU.mult) \
                    .then_inc(bc_done, 1)

            def step(it, s):
                S, n = STEPS * it.b + s, s % 16
                last = it.scan if s else it.scan_before
                gates = n == 1 and (it.scan if s > 16 else it.scan_before)
                for i in range(GT):
                    if it.scan:
                        dve.wait_ge(exp_done, 4 * S + i + 1)
                        dve.wait_ge(mul_done, 4 * S + i + 1)
                        if i == 0:
                            ge(dve, hT_ready, 4 * (S - 1))
                        nc.vector.tensor_tensor_scan(h_sb[:, s % 2, i, :], dA[:, s % 2, i, :], dBx[:, i, :], 0.0,
                                                     ALU.mult, ALU.add).then_inc(scan_done, 1)
                    if gates:
                        gate(it, s, i)
                    elif last:
                        accumulate(it, s, i)
                if gates and last:
                    for tb in range(TB):
                        accumulate(it, s, tb)
                if it.behind and s in (8, 16):
                    add_rows(it, s // 8 - 1, o_added, o_mm)
                if it.behind and 16 <= s < 16 + TB:
                    second_norm(it, s - 16)
                if it.behind and s == FL_AT + 1:
                    scores(it)
                if it.behind and s == FL_AT + 2:
                    choose(it)
                if it.behind and s in (F_AT + 4, F_AT + 8):
                    add_rows(it, (s - F_AT) // 4 - 1, f_added, f_mm)
                if it.ahead and E2_AT < s <= E2_AT + TB:
                    embed_norm(it, s - E2_AT - 1)
                if it.ahead and X_AT + 2 <= s < X_AT + 18:
                    conv(it, s - X_AT - 2)
                if it.ahead and s == BC_AT:
                    project_norms(it)
                if s == 0 and it.scan:
                    if it.scan_before:
                        dve.wait_ge(stt_done, 4 * S)
                    dve.wait_ge(bc_done, it.b + 1)
                    nc.vector.tensor_copy(c_now[:, :, :], bcn[:, :, R + N:E]).then_inc(c_copied, 1)
                    dve.wait_ge(c_copied, it.b + 1)

            run(dve, step, 0, 0)

        @block.scalar
        def _(act):
            act.wait_ge(consts, 16 * NCONST)
            nc.scalar.activation(a_sb[:], a_sb[:], ACT.Exp).then_inc(setup_a, 1)
            act.wait_ge(setup_v, 3)

            def softplus_parts(gn, g, i, bank):
                p, base, tmp = (g + 1) % 2, 2 * (4 * gn + i), sp_tmp[:, i % 2, :]
                ct = 4 * ((g + 1) % GROUPS) + i
                act.wait_ge(dt_mm, 4 * gn + i + 1)
                nc.scalar.activation(dt_sb[:, p, i, :], bank[:, :], ACT.Identity, bias=dtb_sb[:, ct:ct + 1]) \
                    .then_inc(dt_evac, 1)
                act.wait_ge(dt_evac, 4 * gn + i + 1)
                ge(act, dtu_done, 4 * gn + i - 1)
                nc.scalar.activation(tmp, dt_sb[:, p, i, :], ACT.Abs).then_inc(sp_chain, 1)
                act.wait_ge(sp_chain, base + 1)
                nc.scalar.activation(tmp, tmp, ACT.Exp, scale=-1.0).then_inc(sp_chain, 1)
                act.wait_ge(sp_chain, base + 2)
                nc.scalar.activation(tmp, tmp, ACT.Ln, bias=1.0).then_inc(sp_done, 1)

            def b_broadcast(b, s):
                S, n, j = STEPS * b + s, s % 16, s % 4
                if s == 0:
                    act.wait_ge(b_stored, 16 * (b + 1))
                ge(act, mul_done, 4 * (S - 3))
                act.dma_start(b_row[:, j, :], b_dram[bass.ds(b, 1), 0, n * L:(n + 1) * L].to_broadcast([P, L])) \
                    .then_inc(b_loaded[j], 16)

            def step(it, s):
                S, g, n = STEPS * it.b + s, s // 16, s % 16
                G = GROUPS * it.b + g
                if it.scan:
                    for i in range(GT):
                        if n == 0:
                            act.wait_ge(dtu_done, 4 * G + i + 1)
                        ge(act, scan_done, 4 * (S - 2) + i + 1)
                        nc.scalar.activation(dA[:, s % 2, i, :], dt_sb[:, g % 2, i, :], ACT.Exp,
                                             scale=a_sb[:, 4 * g + i, n:n + 1]).then_inc(exp_done, 1)
                if s + 2 < STEPS:
                    if it.scan:
                        b_broadcast(it.b, s + 2)
                elif it.ahead:
                    b_broadcast(it.b + 1, s + 2 - STEPS)

                bb = it.b - 1
                if it.behind and s == 4:
                    if it.ahead_before:
                        for j in range(4):
                            act.wait_ge(cz_stored[j], 16 * 8 * (it.b + 1))
                    act.dma_start(res[:, :, :], h_dram[bass.ds(bb, 1), :, :].rearrange("o (b p) h -> p (o b) h", p=P)) \
                        .then_inc(res_loaded, 16)
                if it.ahead and s == 8:
                    for tb in range(TB):
                        ge(act, low_loaded[tb], 16 * (it.b + 1))
                    act.dma_start(idx[:, :], ids[bass.ds(it.b + 1, 1), :, :].rearrange("o p c -> p (o c)")) \
                        .then_inc(idx_loaded, 16)
                if n == 2 and (it.scan if g < 3 else it.ahead):
                    gn, gi = G + 1, (g + 1) % GROUPS
                    bn = it.b if g < 3 else it.b + 1
                    ge(act, dt_mm, 4 * gn)
                    act.dma_start(dtw_sb[:, :], dtw[:, gi * L:(gi + 1) * L]).then_inc(dtw_loaded, 16)
                    ge(act, mul_done, 64 * (gn - 1))
                    for j in range(4):
                        act.wait_ge(cz_stored[j], 16 * (8 * bn + gi + 1))
                    act.dma_start(u_sb[:, gi % 2, :, :], xc_dram[bass.ds(bn, 1), 4 * gi:4 * gi + 4, :, :]
                                  .rearrange("o i p t -> p (o i) t")).then_inc(u_loaded[gi % 2], 16)
                if n == 14 and it.scan:
                    for p in range(2):
                        ge(act, y_stored[p], 16 * G)
                    for j in range(4):
                        act.wait_ge(cz_stored[j], 16 * (8 * it.b + 4 + g + 1))
                    act.dma_start(xcg[:, :, :], xc_dram[bass.ds(it.b, 1), 4 * g:4 * g + 4, :, :]
                                  .rearrange("o i p t -> p (o i) t")).then_inc(xcg_loaded, 16)
                    act.dma_start(szg[:, :, :], sz_dram[bass.ds(it.b, 1), 4 * g:4 * g + 4, :, :]
                                  .rearrange("o i p t -> p (o i) t")).then_inc(szg_loaded, 16)
                if n in (4, 5) and (it.scan if g else it.scan_before):
                    gp, p = (g - 1) % GROUPS, n - 4
                    by = it.b if g else it.b - 1
                    act.wait_ge(yg_done, 4 * (G - 1) + 2 * p + 2)
                    act.dma_start(y_dram[bass.ds(by, 1), 4 * gp + 2 * p:4 * gp + 2 * p + 2, :, :]
                                  .rearrange("o i p t -> p (o i) t"), szg[:, 2 * p:2 * p + 2, :]) \
                        .then_inc(y_stored[p], 16)
                if it.behind and L3_AT + 1 <= s < L3_AT + 1 + TB:
                    tb = s - L3_AT - 1
                    act.wait_ge(l3_mm, 4 * bb + tb + 1)
                    if tb == 0 and it.ahead_before:
                        act.wait_ge(i_mm, 32 * (it.b + 1))
                    for k in range(2):
                        ins = nc.scalar.activation(hnT[:, 4 * k:4 * k + 4, tb * P:(tb + 1) * P],
                                                   fill_ps[:, 2 * (tb % 2) + k, :].rearrange("p (k t) -> p k t", k=4),
                                                   ACT.Copy)
                    ins.then_inc(l3_evac, 1)
                if it.behind and s == FL_AT + 2:
                    act.wait_ge(shifted, bb + 1)
                    nc.scalar.activation(route[:, 1, :, :], route[:, 0, :, :], ACT.Exp).then_inc(exp_scores, 1)
                if it.behind and s == ROUTE_T_AT + 1:
                    act.wait_ge(rt_mm, bb + 1)
                    if it.ahead_before:
                        act.wait_ge(i_mm, 32 * (it.b + 1))
                    else:
                        act.wait_ge(f_mm, 2 * bb)
                    nc.scalar.activation(xmT[:, :], x_ps[0:LR + 1, :], ACT.Copy).then_inc(rt_evac, 1)
                if it.behind and s == F_AT + 9:
                    act.wait_ge(f_added, 8 * bb + 8)
                    act.dma_start(out[bass.ds(bb, 1), :, :].rearrange("o (b p) h -> p (o b) h", p=P), res[:, :, :]) \
                        .then_inc(out_stored, 16)

                bb = it.b + 1
                if it.ahead and E1_AT + 2 <= s < E1_AT + 2 + TB:
                    tb = s - E1_AT - 2
                    act.wait_ge(e1_mm, 4 * bb + tb + 1)
                    if tb == 0 and it.behind:
                        act.wait_ge(o_mm, 2 * it.b)
                    nc.scalar.activation(lowT[:, tb, :, :], m_ps[:, 0:2 * P].rearrange("p (k t) -> p k t", k=2), ACT.Copy) \
                        .then_inc(e1_evac, 1)
                if it.ahead and E3_AT + 2 <= s < E3_AT + 2 + TB:
                    tb = s - E3_AT - 2
                    act.wait_ge(e3_mm, 4 * bb + tb + 1)
                    if tb == 0:
                        if it.behind:
                            act.wait_ge(f_mm, 2 * it.b)
                        elif it.ahead_before:
                            act.wait_ge(i_mm, 32 * (it.b + 1))
                    for k, bank in enumerate((x_ps, m_ps)):
                        ins = nc.scalar.activation(hnT[:, 4 * k:4 * k + 4, tb * P:(tb + 1) * P],
                                                   bank[:, :].rearrange("p (k t) -> p k t", k=4), ACT.Copy)
                    ins.then_inc(e3_evac, 1)
                if it.ahead and E2_AT + 2 <= s < E2_AT + 2 + TB:
                    tb = s - E2_AT - 2
                    act.wait_ge(e2_norm, 4 * bb + tb + 1)
                    ge(act, h_stored, 16 * (4 * bb + tb))
                    if tb == 0:
                        if it.behind:
                            act.wait_ge(l3_mm, 4 * it.b)
                        ge(act, bc_done, bb)
                    for k in range(2):
                        ins = nc.scalar.activation(h_row[:, k * L:(k + 1) * L], fill_ps[:, 2 * (tb % 2) + k, :], ACT.Copy)
                    ins.then_inc(e2_copied, 1)
                    act.wait_ge(e2_copied, 4 * bb + tb + 1)
                    act.dma_start(h_dram[bass.ds(bb, 1), tb * P:(tb + 1) * P, :].rearrange("o p h -> (o p) h"), h_row[:, :]) \
                        .then_inc(h_stored, 16)
                e = s - X_AT - 2
                if it.ahead and 0 <= e < 16:
                    act.wait_ge(i_mm, 32 * bb + e + 1)
                    if e < 2:
                        if it.behind:
                            act.wait_ge(out_stored, 16 * it.b)
                        ge(act, conv_done, 16 * bb)
                    else:
                        act.wait_ge(conv_done, 16 * bb + e - 1)
                    nc.scalar.activation(xin[:, e % 2, 3:3 + L], fill_ps[:, e % 4, :], ACT.Copy).then_inc(i_evac, 1)
                e = s - X_AT - 4
                if it.ahead and 0 <= e < 16:
                    act.wait_ge(conv_done, 16 * bb + e + 1)
                    nc.scalar.activation(cz[:, e % 4, :], cz[:, e % 4, :], ACT.Silu).then_inc(silu_done, 1)
                    act.wait_ge(silu_done, 16 * bb + e + 1)
                    act.dma_start(xc_dram[bass.ds(bb, 1), e, :, :].rearrange("o p t -> (o p) t"), cz[:, e % 4, :]) \
                        .then_inc(cz_stored[e % 4], 16)
                t, exists, bz = (s - 2, it.ahead, it.b + 1) if s >= 2 else (s + STEPS - 2, it.ahead_before, it.b)
                if exists:
                    for z in z_tiles(t):
                        act.wait_ge(i_mm, 32 * bz + 16 + z + 1)
                        act.wait_ge(cz_stored[z % 4], 16 * (8 * bz + 4 + z // 4))
                        if z < 4:
                            act.wait_ge(xp_mm, 16 * bz + 12 + z + 1)
                        nc.scalar.activation(cz[:, z % 4, :], fill_ps[:, z % 4, :], ACT.Silu).then_inc(i_evac, 1)
                        act.wait_ge(i_evac, 32 * bz + 16 + z + 1)
                        act.dma_start(sz_dram[bass.ds(bz, 1), z, :, :].rearrange("o p t -> (o p) t"), cz[:, z % 4, :]) \
                            .then_inc(cz_stored[z % 4], 16)
                if it.ahead and s == BCT_AT + 1:
                    act.wait_ge(bct_mm, bb + 1)
                    if it.scan:
                        act.wait_ge(dt_mm, 4 * (GROUPS * it.b + 3) + 4)
                        act.wait_ge(b_stored, 16 * bb)
                    nc.scalar.activation(dtB[:, :], m_ps[0:R + N, :], ACT.Copy).then_inc(bct_evac, 1)
                    act.wait_ge(bct_evac, bb + 1)
                    act.dma_start(b_dram[bass.ds(bb, 1), 0, :].rearrange("o (n t) -> (o n) t", n=N), dtB[R:R + N, :]) \
                        .then_inc(b_stored, 16)
                t, exists = (s - 2, (it.scan if (s - 2) // 16 < 3 else it.ahead)) if s >= 2 else (s + STEPS - 2, it.ahead_before)
                if exists:
                    for i in dt_tiles(t):
                        gn = GROUPS * (it.b if s >= 2 else it.b - 1) + t // 16 + 1
                        softplus_parts(gn, t // 16, i, x_ps if t // 16 == 3 and i % 2 else m_ps)

            run(act, step, 0, 0)
            act.wait_ge(out_stored, 16 * NB)


def kernel(**inputs):
    import numpy as _np
    import concourse.bacc as _bacc
    from concourse import mybir as _mybir
    from concourse.bass_utils import run_bass_kernel_spmd as _run

    a = {k: _np.asarray(v) for k, v in inputs.items()}
    p, din, h, low = 128, 2048, 1024, 256
    laid = {
        "ids": a["x"].reshape(8, 4, p).transpose(0, 2, 1),
        "ein": a["L0_tok_E_in"].transpose(1, 0, 2).reshape(-1, low),
        "wout": a["L0_tok_W_out"].transpose(0, 2, 1).reshape(2, p, h).transpose(1, 0, 2),
        "probs_col": _np.repeat(a["L0_tok_probs"], 32).reshape(2, p).T,
        "w_in": a["L0_attn_in_proj_w"].reshape(8, p, 32, p).transpose(2, 1, 0, 3).reshape(32, p, h),
        "conv_w": a["L0_attn_conv_w"].reshape(16, p, 4).transpose(1, 0, 2),
        "conv_b": a["L0_attn_conv_b"].reshape(16, p).T,
        "wx": a["L0_attn_x_proj_w"].T.reshape(16, p, 96).transpose(1, 0, 2),
        "dtw": a["L0_attn_dt_proj_w"].T,
        "dt_bias": a["L0_attn_dt_bias"].reshape(16, p).T,
        "a_log": a["L0_attn_A_log"].reshape(16, p, 16).transpose(1, 0, 2),
        "d_par": a["L0_attn_D_param"].reshape(16, p).T,
        "ln_w": _np.broadcast_to(_np.concatenate([a["L0_attn_dt_ln_w"], a["L0_attn_B_ln_w"], a["L0_attn_C_ln_w"]]), (p, 96)),
        "w_o": a["L0_attn_out_proj_w"].T.reshape(8, 2, p, 2, 512).transpose(3, 0, 2, 1, 4).reshape(16, p, h),
        "w_f": a["L0_ffn_W"].T.reshape(4, 2, p, 2, 512).transpose(3, 0, 2, 1, 4).reshape(8, p, h),
        "ag": _np.concatenate([a["L0_ffn_A"], a["L0_ffn_gate_w"]]).T.reshape(8, p, 68).transpose(1, 0, 2),
        "bt": _np.concatenate([a["L0_ffn_B"].T, a["L0_ffn_b"][None, :]]),
        "gate_b": _np.broadcast_to(a["L0_ffn_gate_b"], (p, 4, 4)),
    }
    nc = _bacc.Bacc("TRN2", target_bir_lowering=False, num_devices=1)
    arrays, args = {}, []
    for name, v in laid.items():
        arrays[name] = _np.ascontiguousarray(v)
        args.append(nc.dram_tensor(name, v.shape, _mybir.dt.from_np(v.dtype), kind="ExternalInput").ap())
    out = nc.dram_tensor("out", (8, 512, h), _mybir.dt.from_np(_np.dtype("float32")), kind="ExternalOutput").ap()
    build(nc, *args, out)
    r = _run(nc, [arrays], core_ids=[0])
    return r.results[0]["out"]
```

```python
from contextlib import ExitStack

import concourse.bass as bass
from concourse import mybir

ALU = mybir.AluOpType
ACT = mybir.ActivationFunctionType
AX = mybir.AxisListType
F32 = mybir.dt.float32
I32 = mybir.dt.int32

P = 128
TB = 4
GT = 4
EPS_LN = 1e-5
EPS_RMS = 1e-6
NEWTON = 3
ROOT_OPS = 2 + 4 * NEWTON
NORM_OPS = 4 + ROOT_OPS + 1

STEPS = 64
E1_AT = 0
E2_AT = (1, 4, 7, 10)
E_NORM_AT = (3, 6, 9, 12)
E3_AT = (3, 6, 9, 12)
STATS_AT = (10, 11, 13, 14)
L2_AT = 19
F_AT = 24
FL_AT = 24
ROUTE_T_AT = 27
X_AT = 34
XP_LAG = 4
BC_AT = 54
BCT_AT = 55
DT_AT = ((4, 7, 10, 13), (9, 10, 11, 12), (9, 10, 11, 12), (9, 10, 11, 12))
DT_LAG = (1, 2, 2, 2)
GATHER_AT = 40

TAIL_AT = 50
TAIL = (3, 3, 2, 2, 4, 2, 2, 2, 2, 2, 2, 2)
TAIL_TILE = 25
TAIL_STEPS = [TAIL_AT + k for k, quarters in enumerate(TAIL) for _ in range(quarters)]
IN_TILES = ([(17 + k, 16 + k) for k in range(7)] + [(32, 23), (33, 24)] + [(X_AT + k, k) for k in range(16)]
            + [(TAIL_STEPS[4 * k + 3], TAIL_TILE + k) for k in range(7)])
IN_AT = {step: e for e, (step, tile) in enumerate(IN_TILES)}


def in_quarters(s, part):
    if s < TAIL_AT:
        return [(IN_AT[s], part)] if s in IN_AT else []
    if s >= TAIL_AT + len(TAIL):
        return []
    parts = {2: (1, 3), 3: (0, 1, 3), 4: (0, 1, 2, 3)}[TAIL[s - TAIL_AT]]
    done = sum(TAIL[:s - TAIL_AT])
    return [divmod(4 * TAIL_TILE + done + parts.index(part), 4)] if part in parts else []


EVAC_AT = [24 if step == 23 else step + 2 for step, tile in IN_TILES]
STREAM = sorted([(t, "O", t) for t in range(16)] + [(F_AT + t, "F", t) for t in range(8)]
                + [(step, "I", e) for e, (step, tile) in enumerate(IN_TILES)])
PLACE = {(kind, k): pos for pos, (step, kind, k) in enumerate(STREAM)}


def dt_tiles(s):
    g, n = s // 16, s % 16
    return [DT_AT[g].index(n)] if n in DT_AT[g] else []


def softplus_tiles(s):
    g, n = s // 16, s % 16 - DT_LAG[s // 16]
    return [DT_AT[g].index(n)] if n in DT_AT[g] else []


def ge(eng, sem, value):
    if isinstance(value, int) and value <= 0:
        return
    eng.wait_ge(sem, value)


class It:

    def __init__(self, b, nb):
        known = isinstance(b, int)
        self.b = b
        self.scan = not known or 0 <= b < nb
        self.behind = not known or 1 <= b <= nb
        self.ahead = not known or b + 1 < nb
        self.scan_before = not known or 0 <= b - 1 < nb
        self.ahead_before = not known or (b >= 0 and b < nb)
        self.ahead2 = not known or b + 2 < nb
        if known:
            self.w_base = [0, 8][b + 1] if b <= 0 else 16 + 14 * min(b - 1, nb - 2) + (6 if b == nb else 0)
        else:
            self.w_base = 16 + 14 * (b - 1)

    def w_slot(self, kind, k):
        return PLACE[kind, k] % 4

    def w_count(self, kind, k):
        pos = PLACE[kind, k]
        return self.w_base + sum(self.ahead if STREAM[p][1] == "I" else self.behind for p in range(pos % 4, pos, 4))


def build(nc, ids, ein, wout, probs_col, w_in, conv_w, conv_b, wx, dtw, dt_bias, a_log, d_par, ln_w,
          w_o, w_f, ag, bt, gate_b, out):
    NB, L, H = out.shape
    DT = conv_w.shape[1]
    KH = H // P
    R = dtw.shape[0]
    N = a_log.shape[2]
    E = wx.shape[2]
    LR = bt.shape[0] - 1
    NR = ag.shape[2] - LR
    GROUPS = DT // GT
    assert GROUPS * N == STEPS and L == TB * P

    h_dram = nc.dram_tensor("h_spill", (NB, L, H), F32, kind="Internal").ap()
    xc_dram = nc.dram_tensor("xc_spill", (NB, DT, P, L), F32, kind="Internal").ap()
    sz_dram = nc.dram_tensor("silu_z_spill", (NB, DT, P, L), F32, kind="Internal").ap()
    y_dram = nc.dram_tensor("y_spill", (NB, DT, P, L), F32, kind="Internal").ap()
    b_dram = nc.dram_tensor("b_rows", (NB, 1, N * L), F32, kind="Internal").ap()

    with ExitStack() as ctx:
        def sb(name, shape, dt=F32):
            return ctx.enter_context(nc.sbuf_tensor(name, shape, dt))

        def psum(name, shape):
            return ctx.enter_context(nc.psum_tensor(name, shape, F32))

        def sem(name):
            return ctx.enter_context(nc.semaphore(name))

        w_ring = sb("w_ring", [P, 4, 1024])
        hnT = sb("hnT", [P, KH, L])
        res = sb("res", [P, TB, H])
        res_flat = res[:, :, :].rearrange("p a b -> p (a b)")
        cz = res_flat[:, 0:2048].rearrange("p (s t) -> p s t", s=4)
        xin = res_flat[:, 2048:2048 + 2 * 516].rearrange("p (s t) -> p s t", s=2)
        h2nT = sb("h2nT", [P, KH, L])
        hn = h2nT[:, 0:2, :].rearrange("p a b -> p (a b)")
        q_reg = sb("q_reg", [P, 2048])
        z_st = q_reg[:, :].rearrange("p (s t) -> p s t", s=4)
        y_in = q_reg[:, :].rearrange("p (s i t) -> p s i t", s=2, i=2)
        h_row = sb("h_row", [P, H])
        low = sb("low", [P, TB, 256])
        lowT = low[:, :, :].rearrange("p b (k t) -> p b k t", k=2)
        xmT = low[0:LR + 1, 0:2, :].rearrange("p a b -> p (a b)")
        idx = sb("idx", [P, TB], I32)
        wout_sb = sb("wout_sb", [P, 2, H])
        wx_sb = sb("wx_sb", [P, DT, E])
        dtw_sb = sb("dtw_sb", [R, L])
        ag_sb = sb("ag_sb", [P, KH, LR + NR])
        bt_sb = sb("bt_sb", [LR + 1, H])
        dt_sb = sb("dt_sb", [P, 2, GT, L])
        u_sb = sb("u_sb", [P, 2, GT, L])
        sp_tmp = sb("sp_tmp", [P, 2, L])
        xcg = sb("xcg", [P, GT, L])
        szg = sb("szg", [P, 2, L])
        dA = sb("dA", [P, GT, L])
        dBx = sb("dBx", [P, GT, L])
        h_sb = sb("h_sb", [P, 2, GT, L])
        b_row = sb("b_row", [P, 4, L])
        y_acc = sb("y_acc", [P, TB, GT * P])
        dtB = sb("dtB", [R + N, L])
        xm = sb("xm", [P, TB, LR + 1])
        bcn = sb("bcn", [P, TB, E])
        c_now = sb("c_now", [P, TB, N])
        a_sb = sb("a_sb", [P, DT, N])
        ident = sb("ident", [P, P])
        zero_sb = dA[:, 0, 0:P]
        cw_sb = sb("cw_sb", [P, DT, 4])
        cb_sb = sb("cb_sb", [P, DT])
        dtb_sb = sb("dtb_sb", [P, DT])
        d_sb = sb("d_sb", [P, DT])
        lnw_sb = sb("lnw_sb", [P, E])
        gb_sb = sb("gb_sb", [P, TB, NR])
        pc_sb = sb("pc_sb", [P, 2])
        stats = sb("stats", [P, 2, 6])
        stats2 = sb("stats2", [P, TB, 2, 6])
        mv2 = sb("mv2", [P, TB, 2])
        rstd2 = sb("rstd2", [P, TB])
        mv = sb("mv", [P, 2])
        rstd = sb("rstd", [P, 1])
        rms = sb("rms", [P, 6, TB])
        rtmp = sb("rtmp", [P, 3 * TB])
        route = sb("route", [P, 3, TB, NR])
        route1 = sb("route1", [P, 4, TB])

        fill_ps = psum("fill_ps", [P, 4, L])
        x_ps = psum("x_ps", [P, L])
        m_ps = psum("m_ps", [P, L])
        hT_ps = psum("hT_ps", [P, 2, L])

        w_loaded = [sem(f"w_loaded{j}") for j in range(4)]
        y_loaded = [sem(f"y_loaded{j}") for j in range(2)]
        y_stored = [sem(f"y_stored{j}") for j in range(2)]
        b_loaded = [sem(f"b_loaded{j}") for j in range(4)]
        u_loaded = [sem(f"u_loaded{j}") for j in range(2)]
        cz_stored = [sem(f"cz_stored{j}") for j in range(4)]
        z_stored = [sem(f"z_stored{j}") for j in range(4)]
        low_loaded = [sem(f"low_loaded{j}") for j in range(TB)]
        xcg_loaded, szg_loaded, dtw_loaded, idx_loaded, res_loaded = (
            sem(n) for n in ("xcg_loaded", "szg_loaded", "dtw_loaded", "idx_loaded", "res_loaded"))
        h_stored, out_stored, b_stored, consts = (sem(n) for n in ("h_stored", "out_stored", "b_stored", "consts"))
        hT_ready, back_mm, dt_mm, o_step, f_step, l3_mm, fl_mm, rt_mm, f_mm, e1_mm, e2_mm, e3_mm, i_mm, xp_mm, bct_mm = (
            sem(n) for n in ("hT_ready", "back_mm", "dt_mm", "o_step", "f_step", "l3_mm", "fl_mm", "rt_mm", "f_mm",
                             "e1_mm", "e2_mm", "e3_mm", "i_mm", "xp_mm", "bct_mm"))
        scan_done, stt_done, gate_done, o_added, f_added, conv_done, e2_norm, h2n_done, shifted, routed, bc_done, c_copied, dt_done = (
            sem(n) for n in ("scan_done", "stt_done", "gate_done", "o_added", "f_added", "conv_done", "e2_norm",
                             "h2n_done", "shifted", "routed", "bc_done", "c_copied", "dt_done"))
        e_chain, l_chain, conv_chain, sh_chain, rt_chain, bc_chain = (
            sem(n) for n in ("e_chain", "l_chain", "conv_chain", "sh_chain", "rt_chain", "bc_chain"))
        setup_v, setup_a, setup_p = sem("setup_v"), sem("setup_a"), sem("setup_p")
        exp_done, e1_evac, e2_copied, e3_evac, l3_evac, i_evac, silu_done, dt_evac, sp_chain, sp_done, exp_scores, rt_evac, bct_evac = (
            sem(n) for n in ("exp_done", "e1_evac", "e2_copied", "e3_evac", "l3_evac", "i_evac", "silu_done",
                             "dt_evac", "sp_chain", "sp_done", "exp_scores", "rt_evac", "bct_evac"))
        mul_done, dtu_done, yg_done = (sem(n) for n in ("mul_done", "dtu_done", "yg_done"))

        NCONST = 12

        def dt_bank(g, i):
            return x_ps if g == 3 and i % 2 else m_ps

        block = ctx.enter_context(nc.Block())

        def run(eng, step, nb=NB):
            for b in (-1, 0):
                for s in range(STEPS):
                    step(It(b, nb), s)
            with eng.Fori(1, nb - 2) as b:
                for s in range(STEPS):
                    step(It(b, nb), s)
            for b in (nb - 2, nb - 1, nb):
                for s in range(STEPS if b < nb else F_AT + 11):
                    step(It(b, nb), s)

        @block.sync
        def _(sp):
            def freed(it, place):
                b, known = it.b, isinstance(it.b, int)
                while not known or b >= -1:
                    if place < 0:
                        place, b = place + len(STREAM), b - 1
                        continue
                    kind, k = STREAM[place][1:]
                    if not known or (It(b, NB).ahead if kind == "I" else It(b, NB).behind):
                        if kind == "I":
                            sp.wait_ge(i_mm, 2 * DT * (b + 1) + k + 1)
                        elif kind == "O":
                            sp.wait_ge(o_step, 16 * (b - 1) + k + 1)
                        else:
                            sp.wait_ge(f_step, 8 * (b - 1) + k + 1)
                        return
                    place -= 4

            def load_w(it, kind, k, src):
                j = it.w_slot(kind, k)
                freed(it, PLACE[kind, k] - 4)
                sp.dma_start(w_ring[:, j, :], src).then_inc(w_loaded[j], 16)

            def step(it, s):
                bb = it.b - 1
                if it.behind and s < 16:
                    load_w(it, "O", s, w_o[s])
                    if s == 0:
                        if it.ahead_before:
                            for j in range(4):
                                sp.wait_ge(z_stored[j], 64 * (it.b + 1))
                        else:
                            sp.wait_ge(o_step, 16 * bb)
                    kp, p = s % 8, s % 2
                    if s >= 2:
                        sp.wait_ge(o_step, 16 * bb + s - 1)
                    ge(sp, y_stored[p], 16 * (4 * bb + kp // 2 + 1))
                    sp.dma_start(y_in[:, p, :, :], y_dram[bass.ds(bb, 1), 2 * kp:2 * kp + 2, :, :]
                                 .rearrange("o i p t -> p (o i) t")).then_inc(y_loaded[p], 16)
                if it.behind and F_AT <= s < F_AT + 8:
                    load_w(it, "F", s - F_AT, w_f[s - F_AT])
                if it.ahead and s in IN_AT:
                    load_w(it, "I", IN_AT[s], w_in[IN_TILES[IN_AT[s]][1]])
                S, g, n = STEPS * it.b + s, s // 16, s % 16
                G = GROUPS * it.b + g
                if it.behind and s == 4:
                    if it.ahead_before:
                        for j in range(4):
                            sp.wait_ge(cz_stored[j], 64 * (it.b + 1))
                        sp.nop(nofuse=True)
                        sp.wait_ge(xp_mm, 16 * (it.b + 1))
                    else:
                        sp.wait_ge(out_stored, 16 * bb)
                    sp.dma_start(res[:, :, :], h_dram[bass.ds(bb, 1), :, :].rearrange("o (b p) h -> p (o b) h", p=P)) \
                        .then_inc(res_loaded, 16)
                if it.ahead2 and s == GATHER_AT - 4:
                    for tb in range(TB):
                        sp.wait_ge(low_loaded[tb], 16 * (it.b + 2))
                    sp.dma_start(idx[:, :], ids[bass.ds(it.b + 2, 1), :, :].rearrange("o p c -> p (o c)")) \
                        .then_inc(idx_loaded, 16)
                if n == 2 and (it.scan if g < 3 else it.ahead):
                    gn, gi = G + 1, (g + 1) % GROUPS
                    bn = it.b if g < 3 else it.b + 1
                    ge(sp, dt_mm, 4 * gn)
                    sp.dma_start(dtw_sb[:, :], dtw[:, gi * L:(gi + 1) * L]).then_inc(dtw_loaded, 16)
                    ge(sp, mul_done, 64 * (gn - 1))
                    for j in range(4):
                        sp.wait_ge(cz_stored[j], 16 * (4 * bn + gi + 1))
                    sp.nop(nofuse=True)
                    sp.dma_start(u_sb[:, gi % 2, :, :], xc_dram[bass.ds(bn, 1), 4 * gi:4 * gi + 4, :, :]
                                  .rearrange("o i p t -> p (o i) t")).then_inc(u_loaded[gi % 2], 16)

                def load_szg(b, g, pair):
                    sp.wait_ge(z_stored[2 * pair], 16 * (4 * b + g + 1))
                    sp.wait_ge(z_stored[2 * pair + 1], 16 * (4 * b + g + 1))
                    sp.dma_start(szg[:, :, :], sz_dram[bass.ds(b, 1), 4 * g + 2 * pair:4 * g + 2 * pair + 2, :, :]
                                  .rearrange("o i p t -> p (o i) t")).then_inc(szg_loaded, 16)

                if n == 14 and it.scan:
                    for p in range(2):
                        ge(sp, y_stored[p], 16 * G)
                    sp.nop(nofuse=True)
                    sp.dma_start(xcg[:, :, :], xc_dram[bass.ds(it.b, 1), 4 * g:4 * g + 4, :, :]
                                  .rearrange("o i p t -> p (o i) t")).then_inc(xcg_loaded, 16)
                    ge(sp, yg_done, 4 * G)
                    sp.nop(nofuse=True)
                    load_szg(it.b, g, 0)
                if n == 2 and (it.scan if g else it.scan_before):
                    gp, by = (g - 1) % GROUPS, it.b if g else it.b - 1
                    sp.wait_ge(yg_done, 4 * (G - 1) + 2)
                    sp.nop(nofuse=True)
                    load_szg(by, gp, 1)

            for dst, src in ((a_sb, a_log), (cw_sb, conv_w), (cb_sb, conv_b), (dtb_sb, dt_bias), (d_sb, d_par),
                             (lnw_sb, ln_w), (gb_sb, gate_b), (pc_sb, probs_col), (wout_sb, wout), (wx_sb, wx),
                             (ag_sb, ag), (bt_sb, bt)):
                sp.dma_start(dst[:], src).then_inc(consts, 16)
            sp.dma_start(idx[:, :], ids[0]).then_inc(idx_loaded, 16)
            run(sp, step)

        @block.gpsimd
        def _(pool):
            nc.gpsimd.memset(zero_sb, 0.0).then_inc(setup_p, 1)
            pool.wait_ge(setup_p, 1)
            nc.gpsimd.affine_select(out=ident[:, :], in_=zero_sb, compare_op=ALU.not_equal, fill=1.0, base=0,
                                    pattern=[[-1, P]], channel_multiplier=1).then_inc(setup_p, 1)
            nc.gpsimd.memset(xm[:], 1.0).then_inc(setup_p, 1)

            def gather(bb, tb):
                if tb == 0:
                    pool.wait_ge(idx_loaded, 16 * (bb + 1))
                ge(pool, e2_mm, 4 * bb)
                if not isinstance(bb, int) or bb >= 3:
                    pool.wait_ge(f_mm, 2 * (bb - 2))
                pool.nop(nofuse=True)
                nc.gpsimd.indirect_dma_start(
                    out=low[:, tb, :], out_offset=None, in_=ein,
                    in_offset=bass.IndirectOffsetOnAxis(ap=idx[:, tb:tb + 1], axis=0)).then_inc(low_loaded[tb], 16)

            def delta(gn, p, i):
                pool.wait_ge(dt_done, 4 * gn + i + 1)
                if i == 0:
                    pool.wait_ge(u_loaded[p], 8 * (gn - p) + 16)
                nc.gpsimd.tensor_tensor(u_sb[:, p, i, :], u_sb[:, p, i, :], dt_sb[:, p, i, :], ALU.mult) \
                    .then_inc(dtu_done, 1)

            def step(it, s):
                S, g, n = STEPS * it.b + s, s // 16, s % 16
                G = GROUPS * it.b + g
                if it.scan:
                    pool.wait_ge(b_loaded[s % 4], 16 * (16 * it.b + s // 4 + 1))
                    for i in range(GT):
                        if n == 0:
                            pool.wait_ge(dtu_done, 4 * G + i + 1)
                        ge(pool, scan_done, 4 * (S - 1) + i + 1)
                        nc.gpsimd.tensor_tensor(dBx[:, i, :], u_sb[:, g % 2, i, :], b_row[:, s % 4, :], ALU.mult) \
                            .then_inc(mul_done, 1)
                if n in (1, 3) and (it.scan if g else it.scan_before):
                    for k in range(2):
                        i = n - 1 + k
                        pool.wait_ge(gate_done, 4 * (G - 1) + i + 1)
                        if k == 0:
                            pool.wait_ge(szg_loaded, 16 * (2 * (G - 1) + n // 2 + 1))
                        nc.gpsimd.tensor_tensor(xcg[:, i, :], xcg[:, i, :], szg[:, k, :], ALU.mult).then_inc(yg_done, 1)
                if n in (13, 15) and (it.scan if g < 3 else it.ahead):
                    for i in (n - 13, n - 12):
                        delta(G + 1, (g + 1) % 2, i)
                if it.ahead2 and GATHER_AT <= s < GATHER_AT + 2 * TB and (s - GATHER_AT) % 2 == 0:
                    gather(it.b + 2, (s - GATHER_AT) // 2)

            for tb in range(TB):
                gather(0, tb)
            run(pool, step)

        @block.tensor
        def _(pe):
            pe.wait_ge(consts, 16 * NCONST)
            pe.wait_ge(setup_p, 3)

            def states_transposed(it, s, tb):
                S, G = STEPS * it.b + s, GROUPS * it.b + s // 16
                if tb == 0:
                    pe.wait_ge(scan_done, 4 * S + 4)
                if s % 16 == 0 and tb < 2:
                    ge(pe, gate_done, 4 * (G - 1) + tb + 3)
                ge(pe, stt_done, 4 * S + tb - 1)
                for i in range(GT):
                    mm = nc.tensor.transpose(hT_ps[:, tb % 2, i * P:(i + 1) * P],
                                             h_sb[:, s % 2, i, tb * P:(tb + 1) * P], ident[:, :])
                mm.then_inc(hT_ready, 1)

            def y_back(it, s, half):
                G = GROUPS * it.b + s // 16
                for i in (2 * half, 2 * half + 1):
                    if i == 0:
                        pe.wait_ge(stt_done, 4 * (STEPS * it.b + s))
                    elif i >= 2:
                        pe.wait_ge(gate_done, 4 * (G - 1) + i - 1)
                    for tb in range(TB):
                        mm = nc.tensor.transpose(hT_ps[:, i % 2, tb * P:(tb + 1) * P], y_acc[:, tb, i * P:(i + 1) * P],
                                                 ident[:, :])
                    mm.then_inc(back_mm, 1)

            def dt_raw(it, s, i):
                g, bb = s // 16, it.b + 1
                gn = GROUPS * it.b + g + 1
                if i == 0:
                    pe.wait_ge(dtw_loaded, 16 * (gn + 1))
                    if g == 1 and it.behind:
                        pe.wait_ge(l3_evac, 4 * (it.b - 1) + 4)
                    elif g == 1 and it.ahead:
                        pe.wait_ge(e3_evac, 4 * bb + 4)
                    if g == 3:
                        pe.wait_ge(bct_evac, bb + 1)
                if g == 0 and it.ahead:
                    pe.wait_ge(e3_evac, 4 * bb + i + 1)
                ge(pe, dt_evac, 4 * gn + i - (g == 3))
                nc.tensor.matmul(dt_bank(g, i)[:, :], dtw_sb[:, i * P:(i + 1) * P], dtB[0:R, :], start=True, stop=True) \
                    .then_inc(dt_mm, 1)

            def out_rows(it, s, m):
                bb, half, kp, p = it.b - 1, s // 8, s % 8, s % 2
                i, tb = m // 4, m % 4
                j = it.w_slot("O", s)
                if m == 0:
                    pe.wait_ge(w_loaded[j], 16 * (it.w_count("O", s) + 1))
                    pe.wait_ge(y_loaded[p], 16 * (8 * bb + s // 2 + 1))
                if kp == 0 and i == 0:
                    if half == 0 and tb == 0 and it.ahead_before:
                        pe.wait_ge(i_evac, 32 * (it.b + 1))
                    elif half == 1:
                        pe.wait_ge(o_added, 8 * bb + tb + 1)
                mm = nc.tensor.matmul(fill_ps[:, tb, :], y_in[:, p, i, tb * P:(tb + 1) * P],
                                      w_ring[:, j, i * L:(i + 1) * L], start=(kp == 0 and i == 0),
                                      stop=(kp == 7 and i == 1))
                if m == 7:
                    mm.then_inc(o_step, 1)

            def dense_rows(it, s, m):
                bb, t = it.b - 1, s - F_AT
                half, kp, i, tb = t // 4, t % 4, m // 4, m % 4
                j = it.w_slot("F", t)
                if m == 0:
                    pe.wait_ge(w_loaded[j], 16 * (it.w_count("F", t) + 1))
                    if t == 0:
                        pe.wait_ge(l3_evac, 4 * bb + 4)
                        if it.ahead:
                            pe.wait_ge(i_evac, 32 * (it.b + 1) + 7)
                if half == 1 and kp == 0 and i == 0:
                    pe.wait_ge(f_added, 8 * bb + tb + 1)
                mm = nc.tensor.matmul(fill_ps[:, tb, :], h2nT[:, 2 * kp + i, tb * P:(tb + 1) * P],
                                      w_ring[:, j, i * L:(i + 1) * L], start=(kp == 0 and i == 0), stop=False)
                if m == 7:
                    mm.then_inc(f_step, 1)

            def low_rank_rows(it, half):
                bb = it.b - 1
                pe.wait_ge(rt_evac, bb + 1)
                for tb in range(TB):
                    mm = nc.tensor.matmul(fill_ps[:, tb, :], xmT[:, tb * P:(tb + 1) * P], bt_sb[:, half * L:(half + 1) * L],
                                          start=False, stop=True)
                mm.then_inc(f_mm, 1)

            def in_rows(it, e, part):
                bb, j, bank = it.b + 1, it.w_slot("I", e), e % 4
                if part == 0:
                    pe.wait_ge(w_loaded[j], 16 * (it.w_count("I", e) + 1))
                    if e == 0:
                        pe.wait_ge(e3_evac, 4 * bb + 4)
                    if e < 4 and it.behind:
                        pe.wait_ge(o_added, 8 * it.b)
                    elif 7 <= e < 11 and it.behind:
                        pe.wait_ge(f_added, 8 * it.b)
                    else:
                        ge(pe, i_evac, 32 * bb + e - 3)
                for k in (2 * part, 2 * part + 1):
                    mm = nc.tensor.matmul(fill_ps[:, bank, :], w_ring[:, j, k * P:(k + 1) * P], hnT[:, k, :],
                                          start=(k == 0), stop=(k == KH - 1))
                if part == 3:
                    mm.then_inc(i_mm, 1)

            def fill(it, s, part):
                if it.behind and s < 16:
                    for m in (2 * part, 2 * part + 1):
                        out_rows(it, s, m)
                if it.behind and F_AT <= s < F_AT + 8:
                    for m in (2 * part, 2 * part + 1):
                        dense_rows(it, s, m)
                if it.ahead:
                    for e, quarter in in_quarters(s, part):
                        in_rows(it, e, quarter)

            def before(it, s):
                bb = it.b - 1
                if it.behind and s == FL_AT:
                    pe.wait_ge(l3_evac, 4 * bb + 4)
                    for tb in range(TB):
                        for k in range(KH):
                            mm = nc.tensor.matmul(x_ps[:, tb * (LR + NR):(tb + 1) * (LR + NR)],
                                                  h2nT[:, k, tb * P:(tb + 1) * P], ag_sb[:, k, :],
                                                  start=(k == 0), stop=(k == KH - 1))
                    mm.then_inc(fl_mm, 1)
                if it.behind and s == ROUTE_T_AT:
                    pe.wait_ge(routed, bb + 1)
                    for tb in range(TB):
                        mm = nc.tensor.transpose(x_ps[0:LR + 1, tb * P:(tb + 1) * P], xm[:, tb, :], ident[:, :])
                    mm.then_inc(rt_mm, 1)
                bb = it.b + 1
                if it.ahead and s == E1_AT:
                    ge(pe, dt_evac, 16 * it.b + 4)
                    for tb in range(TB):
                        pe.wait_ge(low_loaded[tb], 16 * (bb + 1))
                        for k in range(2):
                            mm = nc.tensor.transpose((m_ps if tb < 2 else x_ps)[:, ((tb % 2) * 2 + k) * P:((tb % 2) * 2 + k + 1) * P],
                                                     low[:, tb, k * P:(k + 1) * P], ident[:, :])
                    mm.then_inc(e1_mm, 1)
                x = IN_AT.get(s - XP_LAG, 0)
                c = IN_TILES[x][1]
                if it.ahead and s - XP_LAG in IN_AT and c < 16:
                    pe.wait_ge(silu_done, 16 * bb + c + 1)
                    if c == 0 and it.behind:
                        pe.wait_ge(rt_evac, it.b)
                    for tb in range(TB):
                        mm = nc.tensor.matmul(x_ps[:, tb * E:(tb + 1) * E], cz[:, c % 4, tb * P:(tb + 1) * P],
                                              wx_sb[:, c, :], start=(c == 0 and tb == 0), stop=(c == 15),
                                              skip_group_check=True)
                    mm.then_inc(xp_mm, 1)

            def after(it, s):
                bb = it.b - 1
                if it.behind and s in (F_AT + 3, F_AT + 7):
                    low_rank_rows(it, (s - F_AT) // 4)
                if it.behind and L2_AT <= s < L2_AT + TB:
                    tb = s - L2_AT
                    pe.wait_ge(h2n_done, 4 * bb + tb + 1)
                    if tb:
                        pe.wait_ge(l3_evac, 4 * bb + tb)
                    elif it.ahead:
                        pe.wait_ge(e3_evac, 4 * (it.b + 1) + 4)
                        pe.wait_ge(dt_evac, 16 * it.b + 8)
                    else:
                        pe.wait_ge(rt_evac, bb)
                        pe.wait_ge(dt_evac, min(16 * it.b + 8, 16 * NB))
                    for k in range(KH):
                        mm = nc.tensor.transpose((m_ps if k < 4 else x_ps)[:, (k % 4) * P:(k % 4 + 1) * P],
                                                 h_row[:, k * P:(k + 1) * P], ident[:, :])
                    mm.then_inc(l3_mm, 1)
                bb = it.b + 1
                if it.ahead and s in E2_AT:
                    tb = E2_AT.index(s)
                    if tb == 0:
                        pe.wait_ge(e1_evac, bb + 1)
                    else:
                        pe.wait_ge(e3_evac, 4 * bb + tb)
                    if tb and it.scan:
                        pe.wait_ge(dt_evac, 16 * it.b + 4 + tb)
                    for half, bank in enumerate((m_ps, x_ps)):
                        for k in range(2):
                            mm = nc.tensor.matmul(bank[:, :], lowT[:, tb, k, :], wout_sb[:, k, half * L:(half + 1) * L],
                                                  start=(k == 0), stop=(k == 1))
                    mm.then_inc(e2_mm, 1)
                if it.ahead and s in E3_AT:
                    tb = E3_AT.index(s)
                    pe.wait_ge(e2_norm, 4 * bb + tb + 1)
                    pe.wait_ge(e2_copied, 4 * bb + tb + 1)
                    for k in range(KH):
                        mm = nc.tensor.transpose((m_ps if k < 4 else x_ps)[:, (k % 4) * P:(k % 4 + 1) * P],
                                                 hn[:, k * P:(k + 1) * P], ident[:, :])
                    mm.then_inc(e3_mm, 1)

            def step(it, s):
                before(it, s)
                back = s % 16 == 0 and (it.scan if s else it.scan_before)
                if back:
                    for half in range(2):
                        y_back(it, s, half)
                        fill(it, s, half)
                for tb in range(TB):
                    if it.scan:
                        states_transposed(it, s, tb)
                    if not back:
                        fill(it, s, tb)
                    elif tb in (1, 2):
                        fill(it, s, tb + 1)
                    if tb == 1 and it.ahead and s == BCT_AT:
                        pe.wait_ge(bc_done, it.b + 2)
                        ge(pe, dt_evac, 16 * it.b + 16)
                        for k in range(TB):
                            mm = nc.tensor.transpose(m_ps[0:R + N, k * P:(k + 1) * P], bcn[:, k, 0:R + N], ident[:, :])
                        mm.then_inc(bct_mm, 1)
                    if tb == 1 and (it.scan if s // 16 < 3 else it.ahead):
                        for i in dt_tiles(s):
                            dt_raw(it, s, i)
                after(it, s)

            run(pe, step)

        @block.vector
        def _(dve):
            dve.wait_ge(consts, 16 * NCONST)
            dve.wait_ge(setup_a, 1)
            nc.vector.tensor_scalar(a_sb[:], a_sb[:], -1.0, None, ALU.mult).then_inc(setup_v, 1)

            def linked(chain, at, ins):
                ins.then_inc(chain, 1)
                dve.wait_ge(chain, at)

            def accumulate(it, s, tb):
                S, n = STEPS * it.b + s - 1, (s - 1) % 16
                dve.wait_ge(hT_ready, 4 * S + tb + 1)
                if n == 0:
                    nc.vector.tensor_scalar(y_acc[:, tb, :], hT_ps[:, tb % 2, :], c_now[:, tb, n:n + 1], None, ALU.mult) \
                        .then_inc(stt_done, 1)
                else:
                    dve.wait_ge(stt_done, 4 * (S - 1) + tb + 1)
                    nc.vector.scalar_tensor_tensor(out=y_acc[:, tb, :], in0=hT_ps[:, tb % 2, :],
                                                   scalar=c_now[:, tb, n:n + 1], in1=y_acc[:, tb, :],
                                                   op0=ALU.mult, op1=ALU.add).then_inc(stt_done, 1)

            def gate(it, s, i):
                G = GROUPS * it.b + s // 16 - 1
                gp = (s // 16 - 1) % GROUPS
                dve.wait_ge(back_mm, 4 * G + i + 1)
                if i == 0:
                    dve.wait_ge(xcg_loaded, 16 * (G + 1))
                nc.vector.scalar_tensor_tensor(out=xcg[:, i, :], in0=xcg[:, i, :], scalar=d_sb[:, 4 * gp + i:4 * gp + i + 1],
                                               in1=hT_ps[:, i % 2, :], op0=ALU.mult, op1=ALU.add).then_inc(gate_done, 1)

            def inverse_root(v, y, tmp, chain, at):
                linked(chain, at + 1, nc.vector.tensor_scalar(tmp.bitcast(I32), v.bitcast(I32), 1, None,
                                                              ALU.arith_shift_right))
                linked(chain, at + 2, nc.vector.tensor_scalar(y.bitcast(I32), tmp.bitcast(I32), -1.0, float(0x5F3759DF),
                                                              ALU.mult, ALU.add))
                for k in range(NEWTON):
                    linked(chain, at + 4 * k + 3, nc.vector.tensor_tensor(tmp, y, y, ALU.mult))
                    linked(chain, at + 4 * k + 4, nc.vector.tensor_tensor(tmp, tmp, v, ALU.mult))
                    linked(chain, at + 4 * k + 5, nc.vector.tensor_scalar(tmp, tmp, -0.5, 1.5, ALU.mult, ALU.add))
                    linked(chain, at + 4 * k + 6, nc.vector.tensor_tensor(y, y, tmp, ALU.mult))

            def layernorm(src0, src1, dst, chain, base, last):
                linked(chain, base + 1, nc.vector.bn_stats(stats[:, 0, :], src0))
                linked(chain, base + 2, nc.vector.bn_stats(stats[:, 1, :], src1))
                dve.nop(nofuse=True)
                linked(chain, base + 3, nc.vector.bn_aggr(mv[:, :], stats[:, :, :].rearrange("p a b -> p (a b)")))
                linked(chain, base + 4, nc.vector.tensor_scalar(mv[:, 1:2], mv[:, 1:2], EPS_LN, None, ALU.add))
                inverse_root(mv[:, 1:2], rstd[:, :], rtmp[:, 0:1], chain, base + 4)
                nc.vector.tensor_scalar(dst[:, 0:L], src0, mv[:, 0:1], rstd[:, 0:1], ALU.subtract, ALU.mult) \
                    .then_inc(chain, 1)
                nc.vector.tensor_scalar(dst[:, L:2 * L], src1, mv[:, 0:1], rstd[:, 0:1], ALU.subtract, ALU.mult) \
                    .then_inc(last, 1)
                dve.wait_ge(chain, base + NORM_OPS)

            def softplus_sum(gn, p, pair):
                dve.wait_ge(dt_evac, 4 * gn + 2 * pair + 2)
                dve.wait_ge(sp_done, 2 * gn + pair + 1)
                for k in range(2):
                    raw = dt_sb[:, p, 2 * pair + k, :]
                    nc.vector.scalar_tensor_tensor(out=raw, in0=raw, scalar=0.0, in1=sp_tmp[:, k, :],
                                                   op0=ALU.max, op1=ALU.add).then_inc(dt_done, 1)

            def embed_norm(it, tb):
                bb = it.b + 1
                dve.wait_ge(e2_mm, 4 * bb + tb + 1)
                ge(dve, e3_mm, 4 * bb + tb)
                ge(dve, e2_norm, 4 * bb + tb)
                layernorm(m_ps[:, :], x_ps[:, :], hn, e_chain, NORM_OPS * (4 * bb + tb), e2_norm)

            def second_stats(it, half, blocks):
                bb = it.b - 1
                dve.wait_ge(o_added, 8 * bb + 4 * half + 4)
                for tb in blocks:
                    nc.vector.bn_stats(stats2[:, tb, half, :], res[:, tb, half * L:(half + 1) * L]).then_inc(l_chain, 1)

            def second_moments(it):
                base = (3 * TB + 1 + ROOT_OPS) * (it.b - 1)
                dve.wait_ge(l_chain, base + 2 * TB)
                for tb in range(TB):
                    dve.nop(nofuse=True)
                    nc.vector.bn_aggr(mv2[:, tb, :], stats2[:, tb, :, :].rearrange("p a b -> p (a b)")).then_inc(l_chain, 1)
                dve.wait_ge(l_chain, base + 3 * TB)
                linked(l_chain, base + 3 * TB + 1, nc.vector.tensor_scalar(mv2[:, :, 1], mv2[:, :, 1], EPS_LN, None, ALU.add))
                inverse_root(mv2[:, :, 1], rstd2[:, :], rtmp[:, 0:TB], l_chain, base + 3 * TB + 1)

            def second_norm(it, tb):
                bb = it.b - 1
                if tb:
                    dve.wait_ge(l3_mm, 4 * bb + tb)
                else:
                    dve.wait_ge(h_stored, 16 * 4 * min(it.b + 2, NB) if isinstance(it.b, int) else 64 * (it.b + 2))
                nc.vector.tensor_scalar(h_row[:, :], res[:, tb, :], mv2[:, tb, 0:1], rstd2[:, tb:tb + 1],
                                        ALU.subtract, ALU.mult).then_inc(h2n_done, 1)

            def add_rows(it, half, done, mm, steps):
                bb = it.b - 1
                dve.wait_ge(mm, steps * (2 * bb + half + 1))
                if half == 0:
                    dve.wait_ge(res_loaded, 16 * (bb + 1))
                for tb in range(TB):
                    nc.vector.tensor_tensor(res[:, tb, half * L:(half + 1) * L], res[:, tb, half * L:(half + 1) * L],
                                            fill_ps[:, tb, :], ALU.add).then_inc(done, 1)

            def conv(it, e):
                bb, base = it.b + 1, 4 * (16 * (it.b + 1) + e)
                c = cz[:, e % 4, :]
                x = xin[:, e % 2, :]
                ge(dve, cz_stored[e % 4], 16 * (4 * bb + e // 4))
                ge(dve, xp_mm, 16 * bb + e - 3)
                if e == 0 and it.behind:
                    dve.wait_ge(out_stored, 16 * it.b)
                nc.vector.memset(x[:, 0:3], 0.0).then_inc(conv_chain, 1)
                dve.wait_ge(conv_chain, base + 1)
                dve.wait_ge(i_evac, 32 * bb + IN_AT[X_AT + e] + 1)
                linked(conv_chain, base + 2, nc.vector.tensor_scalar(c, x[:, 0:L], cw_sb[:, e, 0:1], cb_sb[:, e:e + 1],
                                                                     ALU.mult, ALU.add))
                for k in (1, 2):
                    linked(conv_chain, base + 2 + k, nc.vector.scalar_tensor_tensor(
                        out=c, in0=x[:, k:k + L], scalar=cw_sb[:, e, k:k + 1], in1=c, op0=ALU.mult, op1=ALU.add))
                nc.vector.scalar_tensor_tensor(out=c, in0=x[:, 3:3 + L], scalar=cw_sb[:, e, 3:4], in1=c,
                                               op0=ALU.mult, op1=ALU.add).then_inc(conv_done, 1)

            def scores(it):
                bb, base = it.b - 1, 2 * (it.b - 1)
                x = x_ps[:, 0:TB * (LR + NR)].rearrange("p (b c) -> p b c", b=TB)
                dve.wait_ge(fl_mm, bb + 1)
                linked(sh_chain, base + 1, nc.vector.tensor_tensor(route[:, 0, :, :], x[:, :, LR:LR + NR], gb_sb[:, :, :],
                                                                   ALU.add))
                linked(sh_chain, base + 2, nc.vector.tensor_reduce(route1[:, 0, :], route[:, 0, :, :], AX.X, ALU.max))
                nc.vector.tensor_tensor(route[:, 0, :, :], route[:, 0, :, :],
                                        route1[:, 0, :].unsqueeze(2).to_broadcast([P, TB, NR]), ALU.subtract) \
                    .then_inc(shifted, 1)

            def choose(it):
                bb, base = it.b - 1, 10 * (it.b - 1)
                x = x_ps[:, 0:TB * (LR + NR)].rearrange("p (b c) -> p b c", b=TB)
                ex, pr, mk = route[:, 1, :, :], route[:, 0, :, :], route[:, 2, :, :]
                total, top, inv = route1[:, 1, :], route1[:, 2, :], route1[:, 3, :]
                at = [base]

                def then(ins):
                    at[0] += 1
                    linked(rt_chain, at[0], ins)

                dve.wait_ge(exp_scores, bb + 1)
                then(nc.vector.tensor_reduce(total, ex, AX.X, ALU.add))
                then(nc.vector.reciprocal(inv, total))
                then(nc.vector.tensor_tensor(pr, ex, inv.unsqueeze(2).to_broadcast([P, TB, NR]), ALU.mult))
                then(nc.vector.tensor_reduce(top, pr, AX.X, ALU.max))
                then(nc.vector.reciprocal(inv, top))
                then(nc.vector.tensor_tensor(mk[:, :, 0], top, inv, ALU.mult))
                then(nc.vector.tensor_tensor(ex, pr, top.unsqueeze(2).to_broadcast([P, TB, NR]), ALU.is_lt))
                for r in range(1, NR):
                    then(nc.vector.tensor_tensor(mk[:, :, r], mk[:, :, r - 1], ex[:, :, r - 1], ALU.mult))
                if it.ahead_before:
                    dve.wait_ge(i_mm, 32 * (it.b + 1))
                else:
                    dve.wait_ge(rt_mm, bb)
                lo = 0
                for r, hi in enumerate((8, 16, 32, 64)):
                    ins = nc.vector.tensor_tensor(xm[:, :, lo:hi], x[:, :, lo:hi],
                                                  mk[:, :, r:r + 1].to_broadcast([P, TB, hi - lo]), ALU.mult)
                    lo = hi
                ins.then_inc(routed, 1)

            def project_norms(it):
                bb, base = it.b + 1, (5 + ROOT_OPS) * (it.b + 1)
                x = x_ps[:, 0:TB * E].rearrange("p (b c) -> p b c", b=TB)
                sq = h_row[:, 0:TB * E].rearrange("p (b c) -> p b c", b=TB)
                dve.wait_ge(xp_mm, 16 * bb + 16)
                dve.wait_ge(h_stored, 64 * (bb + 1))
                linked(bc_chain, base + 1, nc.vector.tensor_copy(bcn[:, :, :], x))
                linked(bc_chain, base + 2, nc.vector.tensor_tensor(sq, bcn[:, :, :], bcn[:, :, :], ALU.mult))
                cuts = ((0, R), (R, R + N), (R + N, E))
                for k, (lo, hi) in enumerate(cuts):
                    ins = nc.vector.tensor_reduce(rms[:, k, :], sq[:, :, lo:hi], AX.X, ALU.add)
                linked(bc_chain, base + 3, ins)
                for k, (lo, hi) in enumerate(cuts):
                    ins = nc.vector.tensor_scalar(rms[:, k, :], rms[:, k, :], 1.0 / (hi - lo), EPS_RMS, ALU.mult, ALU.add)
                linked(bc_chain, base + 4, ins)
                inverse_root(rms[:, 0:3, :], rms[:, 3:6, :], rtmp[:, :].rearrange("p (a b) -> p a b", a=3), bc_chain, base + 4)
                for k, (lo, hi) in enumerate(cuts):
                    ins = nc.vector.tensor_tensor(sq[:, :, lo:hi], bcn[:, :, lo:hi],
                                                  rms[:, 3 + k, :].unsqueeze(2).to_broadcast([P, TB, hi - lo]), ALU.mult)
                linked(bc_chain, base + 5 + ROOT_OPS, ins)
                nc.vector.tensor_tensor(bcn[:, :, :], sq, lnw_sb[:, :].unsqueeze(1).to_broadcast([P, TB, E]), ALU.mult) \
                    .then_inc(bc_done, 1)

            def step(it, s):
                S, n = STEPS * it.b + s, s % 16
                last = it.scan if s else it.scan_before
                for i in range(GT):
                    if it.scan:
                        dve.wait_ge(exp_done, 4 * S + i + 1)
                        dve.wait_ge(mul_done, 4 * S + i + 1)
                        if i == 0:
                            ge(dve, hT_ready, 4 * (S - 1))
                        nc.vector.tensor_tensor_scan(h_sb[:, s % 2, i, :], dA[:, i, :], dBx[:, i, :], 0.0,
                                                     ALU.mult, ALU.add).then_inc(scan_done, 1)
                    if last:
                        accumulate(it, s, i)
                if it.behind and s == F_AT + 8:
                    add_rows(it, 1, f_added, f_mm, 1)
                if n == 0 and last:
                    for i in range(GT):
                        gate(it, s, i)
                if it.behind and s in (8, 16):
                    add_rows(it, s // 8 - 1, o_added, o_step, 8)
                if it.behind and s in STATS_AT:
                    second_stats(it, 0, (STATS_AT.index(s),))
                if it.behind and s in (17, 18):
                    second_stats(it, 1, (2 * (s - 17), 2 * (s - 17) + 1))
                if it.behind and s == 18:
                    second_moments(it)
                if it.behind and L2_AT <= s < L2_AT + TB:
                    second_norm(it, s - L2_AT)
                if it.behind and s == FL_AT + 1:
                    scores(it)
                if it.behind and s == FL_AT + 2:
                    choose(it)
                if it.behind and s == F_AT + 4:
                    add_rows(it, 0, f_added, f_mm, 1)
                if it.ahead and s in E_NORM_AT:
                    embed_norm(it, E_NORM_AT.index(s))
                if it.scan if s // 16 < 3 else it.ahead:
                    for i in softplus_tiles(s):
                        if i % 2:
                            softplus_sum(GROUPS * it.b + s // 16 + 1, (s // 16 + 1) % 2, i // 2)
                if it.ahead and 0 <= s - 2 - X_AT < 16:
                    conv(it, s - 2 - X_AT)
                if it.ahead and s == BC_AT:
                    project_norms(it)
                if s == 0 and it.scan:
                    if it.scan_before:
                        dve.wait_ge(stt_done, 4 * S)
                    dve.wait_ge(bc_done, it.b + 1)
                    nc.vector.tensor_copy(c_now[:, :, :], bcn[:, :, R + N:E]).then_inc(c_copied, 1)
                    dve.wait_ge(c_copied, it.b + 1)

            run(dve, step)

        @block.scalar
        def _(act):
            act.wait_ge(consts, 16 * NCONST)
            nc.scalar.activation(a_sb[:], a_sb[:], ACT.Exp).then_inc(setup_a, 1)
            act.wait_ge(setup_v, 1)
            

            def softplus_parts(gn, g, i):
                p, base, tmp = (g + 1) % 2, 2 * (4 * gn + i), sp_tmp[:, i % 2, :]
                ct = 4 * ((g + 1) % GROUPS) + i
                act.wait_ge(dt_mm, 4 * gn + i + 1)
                nc.scalar.activation(dt_sb[:, p, i, :], dt_bank(g, i)[:, :], ACT.Identity, bias=dtb_sb[:, ct:ct + 1]) \
                    .then_inc(dt_evac, 1)
                act.wait_ge(dt_evac, 4 * gn + i + 1)
                ge(act, dt_done, 4 * gn + 2 * (i // 2))
                nc.scalar.activation(tmp, dt_sb[:, p, i, :], ACT.Abs).then_inc(sp_chain, 1)
                act.wait_ge(sp_chain, base + 1)
                nc.scalar.activation(tmp, tmp, ACT.Exp, scale=-1.0).then_inc(sp_chain, 1)
                if i % 2:
                    act.wait_ge(sp_chain, base + 2)
                    nc.scalar.activation(sp_tmp[:, :, :], sp_tmp[:, :, :], ACT.Ln, bias=1.0).then_inc(sp_done, 1)

            def b_broadcast(b, s):
                S, n, j = STEPS * b + s, s % 16, s % 4
                if s == 0:
                    act.wait_ge(b_stored, 16 * (b + 1))
                ge(act, mul_done, 4 * (S - 3))
                act.dma_start(b_row[:, j, :], b_dram[bass.ds(b, 1), 0, n * L:(n + 1) * L].to_broadcast([P, L])) \
                    .then_inc(b_loaded[j], 16)

            def step(it, s):
                S, g, n = STEPS * it.b + s, s // 16, s % 16
                G = GROUPS * it.b + g
                if it.scan:
                    for i in range(GT):
                        if n == 0:
                            act.wait_ge(dt_done, 4 * G + i + 1)
                        ge(act, scan_done, 4 * (S - 1) + i + 1)
                        nc.scalar.activation(dA[:, i, :], dt_sb[:, g % 2, i, :], ACT.Exp,
                                             scale=a_sb[:, 4 * g + i, n:n + 1]).then_inc(exp_done, 1)
                if it.behind and L2_AT + 2 <= s < L2_AT + 2 + TB:
                    tb, bb = s - L2_AT - 2, it.b - 1
                    act.wait_ge(l3_mm, 4 * bb + tb + 1)
                    for k, bank in enumerate((m_ps, x_ps)):
                        ins = nc.scalar.activation(h2nT[:, 4 * k:4 * k + 4, tb * P:(tb + 1) * P],
                                                   bank[:, :].rearrange("p (k t) -> p k t", k=4), ACT.Copy)
                    ins.then_inc(l3_evac, 1)
                if it.ahead and s - 2 in E3_AT:
                    tb, bb = E3_AT.index(s - 2), it.b + 1
                    act.wait_ge(e3_mm, 4 * bb + tb + 1)
                    if tb == 0 and it.ahead_before:
                        act.wait_ge(i_mm, 32 * (it.b + 1))
                    for k, bank in enumerate((m_ps, x_ps)):
                        ins = nc.scalar.activation(hnT[:, 4 * k:4 * k + 4, tb * P:(tb + 1) * P],
                                                   bank[:, :].rearrange("p (k t) -> p k t", k=4), ACT.Copy)
                    ins.then_inc(e3_evac, 1)
                if it.behind and s == ROUTE_T_AT + 1:
                    act.wait_ge(rt_mm, it.b)
                    if it.ahead:
                        act.wait_ge(e2_mm, 4 * (it.b + 2))
                    nc.scalar.activation(xmT[:, :], x_ps[0:LR + 1, :], ACT.Copy).then_inc(rt_evac, 1)
                if it.ahead and s == BCT_AT + 2:
                    act.wait_ge(bct_mm, it.b + 2)
                    ge(act, b_stored, 16 * (it.b + 1))
                    nc.scalar.activation(dtB[:, :], m_ps[0:R + N, :], ACT.Copy).then_inc(bct_evac, 1)
                    act.wait_ge(bct_evac, it.b + 2)
                    act.dma_start(b_dram[bass.ds((it.b + 1), 1), 0, :].rearrange("o (n t) -> (o n) t", n=N), dtB[R:R + N, :]) \
                        .then_inc(b_stored, 16)
                if it.scan if g < 3 else it.ahead:
                    for i in softplus_tiles(s):
                        softplus_parts(G + 1, g, i)
                if s + 2 < STEPS:
                    if it.scan:
                        b_broadcast(it.b, s + 2)
                elif it.ahead:
                    b_broadcast(it.b + 1, s + 2 - STEPS)

                bb = it.b - 1
                if n in (2, 4) and (it.scan if g else it.scan_before):
                    gp, p = (g - 1) % GROUPS, n // 2 - 1
                    by = it.b if g else it.b - 1
                    act.wait_ge(yg_done, 4 * (G - 1) + 2 * p + 2)
                    act.dma_start(y_dram[bass.ds(by, 1), 4 * gp + 2 * p:4 * gp + 2 * p + 2, :, :]
                                  .rearrange("o i p t -> p (o i) t"), xcg[:, 2 * p:2 * p + 2, :]) \
                        .then_inc(y_stored[p], 16)
                if it.behind and s == FL_AT + 2:
                    act.wait_ge(shifted, bb + 1)
                    nc.scalar.activation(route[:, 1, :, :], route[:, 0, :, :], ACT.Exp).then_inc(exp_scores, 1)
                if it.behind and s == F_AT + 9:
                    act.wait_ge(f_added, 8 * bb + 8)
                    act.dma_start(out[bass.ds(bb, 1), :, :].rearrange("o (b p) h -> p (o b) h", p=P), res[:, :, :]) \
                        .then_inc(out_stored, 16)

                bb = it.b + 1
                if it.ahead and s == E1_AT + 1:
                    act.wait_ge(e1_mm, bb + 1)
                    for k in range(2):
                        for half, bank in enumerate((m_ps, x_ps)):
                            ins = nc.scalar.activation(lowT[:, 2 * half:2 * half + 2, k, :],
                                                       bank[:, :].rearrange("p (b k t) -> p b k t", b=2, k=2)[:, :, k, :],
                                                       ACT.Copy, scale=pc_sb[:, k:k + 1])
                    ins.then_inc(e1_evac, 1)
                if it.ahead and s - 1 in E_NORM_AT:
                    tb = E_NORM_AT.index(s - 1)
                    act.wait_ge(e2_norm, 4 * bb + tb + 1)
                    ge(act, h_stored, 16 * (4 * bb + tb))
                    if tb == 0:
                        ge(act, bc_done, bb)
                    for k, bank in enumerate((m_ps, x_ps)):
                        ins = nc.scalar.activation(h_row[:, k * L:(k + 1) * L], bank[:, :], ACT.Copy)
                    ins.then_inc(e2_copied, 1)
                    act.wait_ge(e2_copied, 4 * bb + tb + 1)
                    act.dma_start(h_dram[bass.ds(bb, 1), tb * P:(tb + 1) * P, :].rearrange("o p h -> (o p) h"), h_row[:, :]) \
                        .then_inc(h_stored, 16)
                for e in (e for e in range(2 * DT) if it.ahead and EVAC_AT[e] == s):
                    c = IN_TILES[e][1]
                    act.wait_ge(i_mm, 32 * bb + e + 1)
                    if c < 16:
                        ge(act, conv_done, 16 * bb + c - 1)
                        if c < 2 and it.behind:
                            act.wait_ge(out_stored, 16 * it.b)
                        nc.scalar.activation(xin[:, c % 2, 3:3 + L], fill_ps[:, e % 4, :], ACT.Copy).then_inc(i_evac, 1)
                    else:
                        z = c - 16
                        ge(act, z_stored[z % 4], 16 * (4 * bb + z // 4))
                        if z < 4 and it.behind:
                            act.wait_ge(o_step, 16 * it.b)
                        nc.scalar.activation(z_st[:, z % 4, :], fill_ps[:, e % 4, :], ACT.Silu).then_inc(i_evac, 1)
                        act.wait_ge(i_evac, 32 * bb + e + 1)
                        act.dma_start(sz_dram[bass.ds(bb, 1), z, :, :].rearrange("o p t -> (o p) t"), z_st[:, z % 4, :]) \
                            .then_inc(z_stored[z % 4], 16)
                if it.ahead and 0 <= s - 3 - X_AT < 16:
                    c = s - 3 - X_AT
                    act.wait_ge(conv_done, 16 * bb + c + 1)
                    nc.scalar.activation(cz[:, c % 4, :], cz[:, c % 4, :], ACT.Silu).then_inc(silu_done, 1)
                    act.wait_ge(silu_done, 16 * bb + c + 1)
                    act.dma_start(xc_dram[bass.ds(bb, 1), c, :, :].rearrange("o p t -> (o p) t"), cz[:, c % 4, :]) \
                        .then_inc(cz_stored[c % 4], 16)
            run(act, step)
            act.wait_ge(out_stored, 16 * NB)


def kernel(**inputs):
    import numpy as _np
    import concourse.bacc as _bacc
    from concourse import mybir as _mybir
    from concourse.bass_utils import run_bass_kernel_spmd as _run

    a = {k: _np.asarray(v) for k, v in inputs.items()}
    p, din, h, low = 128, 2048, 1024, 256
    laid = {
        "ids": a["x"].reshape(8, 4, p).transpose(0, 2, 1),
        "ein": a["L0_tok_E_in"].transpose(1, 0, 2).reshape(-1, low),
        "wout": a["L0_tok_W_out"].transpose(0, 2, 1).reshape(2, p, h).transpose(1, 0, 2),
        "probs_col": _np.repeat(a["L0_tok_probs"], 32).reshape(2, p).T,
        "w_in": a["L0_attn_in_proj_w"].reshape(8, p, 32, p).transpose(2, 1, 0, 3).reshape(32, p, h),
        "conv_w": a["L0_attn_conv_w"].reshape(16, p, 4).transpose(1, 0, 2),
        "conv_b": a["L0_attn_conv_b"].reshape(16, p).T,
        "wx": a["L0_attn_x_proj_w"].T.reshape(16, p, 96).transpose(1, 0, 2),
        "dtw": a["L0_attn_dt_proj_w"].T,
        "dt_bias": a["L0_attn_dt_bias"].reshape(16, p).T,
        "a_log": a["L0_attn_A_log"].reshape(16, p, 16).transpose(1, 0, 2),
        "d_par": a["L0_attn_D_param"].reshape(16, p).T,
        "ln_w": _np.broadcast_to(_np.concatenate([a["L0_attn_dt_ln_w"], a["L0_attn_B_ln_w"], a["L0_attn_C_ln_w"]]), (p, 96)),
        "w_o": a["L0_attn_out_proj_w"].T.reshape(8, 2, p, 2, 512).transpose(3, 0, 2, 1, 4).reshape(16, p, h),
        "w_f": a["L0_ffn_W"].T.reshape(4, 2, p, 2, 512).transpose(3, 0, 2, 1, 4).reshape(8, p, h),
        "ag": _np.concatenate([a["L0_ffn_A"], a["L0_ffn_gate_w"]]).T.reshape(8, p, 68).transpose(1, 0, 2),
        "bt": _np.concatenate([a["L0_ffn_B"].T, a["L0_ffn_b"][None, :]]),
        "gate_b": _np.broadcast_to(a["L0_ffn_gate_b"], (p, 4, 4)),
    }
    nc = _bacc.Bacc("TRN2", target_bir_lowering=False, num_devices=1)
    arrays, args = {}, []
    for name, v in laid.items():
        arrays[name] = _np.ascontiguousarray(v)
        args.append(nc.dram_tensor(name, v.shape, _mybir.dt.from_np(v.dtype), kind="ExternalInput").ap())
    out = nc.dram_tensor("out", (8, 512, h), _mybir.dt.from_np(_np.dtype("float32")), kind="ExternalOutput").ap()
    build(nc, *args, out)
    r = _run(nc, [arrays], core_ids=[0])
    return r.results[0]["out"]
```
